# Optimizing a Trainium2 kernel written in Bass

```python
import numpy as np
import jax
import jax.numpy as jnp

def _softmax(x, axis=-1):
    return jax.nn.softmax(x, axis=axis)

def _gelu(x):
    return jax.nn.gelu(x, approximate=True)

def _silu(x):
    return jax.nn.silu(x)

def _sigmoid(x):
    return jax.nn.sigmoid(x)

def _layernorm(x, axis=-1, eps=1e-05):
    m = jnp.mean(x, axis=axis, keepdims=True)
    v = jnp.var(x, axis=axis, keepdims=True)
    return (x - m) / jnp.sqrt(v + eps)

def _scatter_add(tgt, idx, src, axis=0):
    return tgt.at[idx].add(src)

def _segment_sum(src, seg, n):
    return jax.ops.segment_sum(src, seg, n)
kernel_name = 'mk_gnn_resnorm_d1_gnn_r8_d41a4d'

def setup_inputs(seed: int=0):
    np.random.seed(seed)
    _w = jnp.asarray

    def _rec_inputs():
        import jax
        import jax.numpy as jnp
        _gk = jax.random.key(seed)
        x = -0.0001978 + 0.9998 * jax.random.normal(jax.random.fold_in(_gk, 1), (12500, 64), jnp.float32)
        _s = jax.random.randint(jax.random.fold_in(_gk, 2), (100000,), 0, 12500, jnp.int32)
        _d = jax.random.randint(jax.random.fold_in(_gk, 3), (100000,), 0, 12500, jnp.int32)
        _loop = jnp.arange(12500, dtype=jnp.int32)
        src = jnp.concatenate([_s, _d, _loop])
        dst = jnp.concatenate([_d, _s, _loop])
        _o = jnp.argsort(dst, stable=True)
        src = src[_o]
        dst = dst[_o]
        edge_attr_64 = 5.93493e-05 + 1.00006 * jax.random.normal(jax.random.fold_in(_gk, 11), (212500, 64), jnp.float32)
        return (x, src, dst, edge_attr_64)
    x, src, dst, edge_attr_64 = _rec_inputs()

    def _L0_gnn_setup():
        import jax, jax.numpy as jnp
        import numpy as np
        N = 12500
        E = 150000
        D = 64

        def leaky_relu(x, slope=0.2):
            return jnp.where(x >= 0, x, slope * x)
        key = jax.random.key(seed)
        ks = jax.random.split(key, 10)
        indices = jax.random.randint(ks[0], (2, E), 0, N, dtype=jnp.int64)
        features = jax.random.normal(ks[1], (N, D), dtype=jnp.float32)
        e_r = jax.random.normal(ks[2], (E, D), dtype=jnp.float32)
        s = 1.0 / np.sqrt(D)
        W1_w = jax.random.normal(ks[3], (D, D), dtype=jnp.float32) * s
        W1_b = jax.random.normal(ks[4], (D,), dtype=jnp.float32) * s
        W2_w = jax.random.normal(ks[5], (D, D), dtype=jnp.float32) * s
        W2_b = jax.random.normal(ks[6], (D,), dtype=jnp.float32) * s
        Watt_w = jax.random.normal(ks[7], (D, D), dtype=jnp.float32) * s
        Watt_b = jax.random.normal(ks[8], (D,), dtype=jnp.float32) * s
        return {'indices': indices, 'features': features, 'e_r': e_r, 'num_nodes': N, 'W1_w': W1_w, 'W1_b': W1_b, 'W2_w': W2_w, 'W2_b': W2_b, 'Watt_w': Watt_w, 'Watt_b': Watt_b}
    _L0_gnn_all = _L0_gnn_setup()
    _L0_gnn_in = {k: v for k, v in _L0_gnn_all.items() if k in ('W1_w', 'W1_b', 'W2_w', 'W2_b', 'Watt_w', 'Watt_b')}
    del _L0_gnn_all
    return {'x': x, 'src': src, 'dst': dst, 'edge_attr_64': edge_attr_64, 'L0_gnn_W1_w': _L0_gnn_in['W1_w'], 'L0_gnn_W1_b': _L0_gnn_in['W1_b'], 'L0_gnn_W2_w': _L0_gnn_in['W2_w'], 'L0_gnn_W2_b': _L0_gnn_in['W2_b'], 'L0_gnn_Watt_w': _L0_gnn_in['Watt_w'], 'L0_gnn_Watt_b': _L0_gnn_in['Watt_b']}

def reference(x, src, dst, edge_attr_64, L0_gnn_W1_w, L0_gnn_W1_b, L0_gnn_W2_w, L0_gnn_W2_b, L0_gnn_Watt_w, L0_gnn_Watt_b):
    import jax
    import jax.numpy as jnp

    def _L0_gnn_ref(indices, features, e_r, num_nodes, W1_w, W1_b, W2_w, W2_b, Watt_w, Watt_b):
        import jax, jax.numpy as jnp
        import numpy as np
        N = 12500
        E = 150000
        D = 64

        def leaky_relu(x, slope=0.2):
            return jnp.where(x >= 0, x, slope * x)
        src, dst = (indices[0], indices[1])
        out_dim = Watt_w.shape[0]
        h_trans = features @ Watt_w.T + Watt_b
        h_src = h_trans[src]
        h_dst = h_trans[dst]
        e_raw = jnp.sum(h_dst * jnp.tanh(h_src + e_r), axis=-1, keepdims=True)
        scaling = 1.0 / out_dim ** 0.5
        e_ij = leaky_relu(e_raw * scaling).astype(jnp.float32)
        max_score = jax.ops.segment_max(jax.lax.stop_gradient(e_ij), dst, num_segments=num_nodes)
        exp_e = jnp.exp(e_ij - max_score[dst])
        denom = jax.ops.segment_sum(exp_e, dst, num_segments=num_nodes)
        alpha = exp_e / (denom[dst] + 1e-09)
        weighted_msg = features[src] * alpha.astype(features.dtype)
        h_neigh = jax.ops.segment_sum(weighted_msg, dst, num_segments=num_nodes)
        sum_h = features + h_neigh
        prod_h = features * h_neigh
        h_out = leaky_relu(sum_h @ W1_w.T + W1_b + (prod_h @ W2_w.T + W2_b))
        return h_out
    edge_index = jnp.stack([src, dst])
    x = _layernorm(x + _L0_gnn_ref(edge_index, x, edge_attr_64, 12500, L0_gnn_W1_w, L0_gnn_W1_b, L0_gnn_W2_w, L0_gnn_W2_b, L0_gnn_Watt_w, L0_gnn_Watt_b), axis=-1)
    return x

_drawn_inputs = setup_inputs


def setup_inputs(seed=0):
    import zlib

    import numpy as np

    out = dict(_drawn_inputs(seed))
    spreads = {}
    factors = {'L0_gnn_Watt_b': 4.767}
    for name, (base, spread) in spreads.items():
        noise = np.random.default_rng([zlib.crc32(name.encode()), seed]).standard_normal(out[name].shape)
        drawn = base * np.exp(spread * noise) if base else spread * noise
        out[name] = jnp.asarray(drawn.astype(out[name].dtype))
    for name, factor in factors.items():
        out[name] = (out[name] * factor).astype(out[name].dtype)
    return out
```

```python
from contextlib import ExitStack

import concourse.bass as bass
from concourse import mybir

ALU = mybir.AluOpType
ACT = mybir.ActivationFunctionType
AX = mybir.AxisListType
F32 = mybir.dt.float32
BF16 = mybir.dt.bfloat16
I32 = mybir.dt.int32

P = 128
MAIN = 16
TAIL = 3
TILES = MAIN + TAIL
CHUNK = 4
SEARCH_ROW = 1700
STEP = 7
MASKED = float(2 ** 100)
LOWEST = -3.0e38
SLOPE = 0.2
EPS_ALPHA = 1e-9
EPS_NORM = 1e-5


def gnn_layer(nc, x, src, dst, edge_attr, w1, b1, w2, b2, watt, batt, out):
    N, D = x.shape
    E, = src.shape
    BLOCKS = (N + P - 1) // P
    LAST_NODES = N - (BLOCKS - 1) * P
    WINDOW = TILES * P
    ROWS = E // SEARCH_ROW
    STEPS = BLOCKS // STEP
    CHUNKS = [range(a, min(a + CHUNK, TILES)) for a in range(0, TILES, CHUNK)]
    NC = len(CHUNKS)
    LOADS = 6
    assert D == 64 and ROWS * SEARCH_ROW == E and STEPS * STEP == BLOCKS
    assert BLOCKS % 2 == 0 and BLOCKS + 1 <= P and ROWS <= P and E >= WINDOW

    with ExitStack() as ctx:
        def sb(name, shape, dt=F32):
            return ctx.enter_context(nc.sbuf_tensor(name, shape, dt))

        def bank(name, dt=F32):
            return ctx.enter_context(nc.psum_tensor(name, [P, 512 * 4 // mybir.dt.size(dt)], dt))

        def sem(name):
            return ctx.enter_context(nc.semaphore(name))

        table = nc.dram_tensor("table", (N, 2 * D), F32, kind="Internal").ap()

        ident = sb("ident", [P, P])
        ident16 = sb("ident16", [P, P], BF16)
        iota_h = sb("iota_h", [P, P], BF16)
        iota_i = sb("iota_i", [P, P], I32)
        sel = sb("sel", [3 * TILES, TILES, P], BF16)
        x_sb = sb("x_sb", [P, BLOCKS, D])
        y_sb = sb("y_sb", [P, BLOCKS, D])
        h3 = sb("h3", [P, BLOCKS, 3, D], BF16)
        stats = sb("stats", [P, BLOCKS, 2])
        watt_sb = sb("watt_sb", [D, D])
        wattT = sb("wattT", [D, D])
        w12 = sb("w12", [D, 2, D])
        w12T = sb("w12T", [P, D])
        w_stage = sb("w_stage", [D, 2 * D])
        batt_bc = sb("batt_bc", [P, D])
        b1_bc = sb("b1_bc", [P, D])
        b2_bc = sb("b2_bc", [P, D])
        b12 = sb("b12", [P, D])
        eps_col = sb("eps_col", [P, 1])
        ones = sb("ones", [P, 1])

        rows_i = sb("rows_i", [P, SEARCH_ROW], I32)
        bound_i = sb("bound_i", [P, 1], I32)
        bound = sb("bound", [P, 1])
        bound_row_i = sb("bound_row_i", [P, P], I32)
        bound_row = sb("bound_row", [P, P])
        row_last = sb("row_last", [P, 1])
        below_row = sb("below_row", [P, P])
        row_f = sb("row_f", [P, 1])
        row_idx = sb("row_idx", [P, 1], I32)
        below = sb("below", [P, SEARCH_ROW])
        below_n = sb("below_n", [P, 1])
        first = sb("first", [P, 1])
        first_row = sb("first_row", [1, P])
        start_row = sb("start_row", [1, P])
        count_row = sb("count_row", [1, P])
        start_i = sb("start_i", [1, P], I32)
        count_i = sb("count_i", [1, P], I32)

        src_i = [sb(f"src_i{q}", [P, TILES], I32) for q in range(2)]
        dst_i = [sb(f"dst_i{q}", [P, TILES], I32) for q in range(2)]
        edge = [sb(f"edge{q}", [P, TILES, D]) for q in range(2)]
        got = [sb(f"got{q}", [P, TILES, 2 * D + 1]) for q in range(2)]
        base = sb("base", [P, 1])
        dst_rel = [sb(f"dst_rel{q}", [P, TILES]) for q in range(2)]
        mask = [sb(f"mask{q}", [P, TILES, P], BF16) for q in range(2)]
        maskT = [sb(f"maskT{q}", [P, TILES, P], BF16) for q in range(2)]
        hotT = [sb(f"hotT{q}", [P, TILES, P], BF16) for q in range(2)]
        raw = [sb(f"raw{q}", [P, TILES]) for q in range(2)]
        scaled = sb("scaled", [P, TILES])
        score = sb("score", [P, TILES])
        score3 = sb("score3", [P, TILES, 3], BF16)
        rest1 = sb("rest1", [P, TILES])
        rest2 = sb("rest2", [P, TILES])
        score3T = sb("score3T", [3 * TILES, P], BF16)
        chunk_max = sb("chunk_max", [P, NC])
        node_max = sb("node_max", [P, 1])
        max3 = sb("max3", [P, 3], BF16)
        mrest1 = sb("mrest1", [P, 1])
        mrest2 = sb("mrest2", [P, 1])
        edge_max = sb("edge_max", [P, TILES])
        arg = sb("arg", [P, TILES])
        weight = sb("weight", [P, TILES, P])
        den = sb("den", [P, 1])
        rden = sb("rden", [P, 1])
        h_neigh = sb("h_neigh", [P, D])
        sum_prod = sb("sum_prod", [P, 2 * D])
        sum_prodT = sb("sum_prodT", [P, P])
        z1 = sb("z1", [P, D])
        z2 = sb("z2", [P, D])
        y_new = sb("y_new", [P, D])
        mean_var = sb("mean_var", [P, 2])
        bn6 = sb("bn6", [P, 6])
        std = sb("std", [P, BLOCKS])
        rstd = sb("rstd", [P, BLOCKS])
        xT = sb("xT", [D, STEP, P])

        ps_hd = [bank(f"ps_hd{i}") for i in range(2)]
        ps_maskT = [bank(f"ps_maskT{i}", BF16) for i in range(2)]
        ps_sc = [bank(f"ps_sc{i}") for i in range(2)]
        ps_acc = bank("ps_acc")
        ps_misc = bank("ps_misc")
        m_sT = ps_misc[0:3 * TILES, 384:384 + P // 2].bitcast(BF16)
        m_max = ps_misc[:, 64:64 + 3 * TILES]
        m_spT = ps_misc[:, 128:256]
        m_out = ps_misc[:, 256:256 + D]

        def by_chunk(name):
            return [sem(f"{name}_{c}") for c in range(NC)]

        w_in = sem("w_in")
        x_in = sem("x_in")
        rows_in = sem("rows_in")
        x_copied = sem("x_copied")
        pool_c = sem("pool_c")
        dve_c = sem("dve_c")
        wT_ps = sem("wT_ps")
        w_ready = sem("w_ready")
        rows_counted = sem("rows_counted")
        row_ready = sem("row_ready")
        rows_got = sem("rows_got")
        below_ready = sem("below_ready")
        first_ready = sem("first_ready")
        first_ps = sem("first_ps")
        windows_ready = sem("windows_ready")
        xT_ps = sem("xT_ps")
        xT_sb = sem("xT_sb")
        h_ps = sem("h_ps")
        h_sb = sem("h_sb")
        h_out = sem("h_out")
        h3_ready = sem("h3_ready")
        loaded = [sem(f"loaded{q}") for q in range(2)]
        gathered = [[sem(f"gathered{q}_{c}") for c in range(NC)] for q in range(2)]
        mask_built = by_chunk("mask_built")
        maskT_ps = by_chunk("maskT_ps")
        maskT_sb = by_chunk("maskT_sb")
        hd_ready = by_chunk("hd_ready")
        hd_used = by_chunk("hd_used")
        added = by_chunk("added")
        tanh_done = by_chunk("tanh_done")
        scored = by_chunk("scored")
        split_done = sem("split_done")
        sT_ps = sem("sT_ps")
        sT_sb = sem("sT_sb")
        sc_ready = by_chunk("sc_ready")
        sc_used = by_chunk("sc_used")
        max_split = sem("max_split")
        max_ps = sem("max_ps")
        arg_done = sem("arg_done")
        weights_done = by_chunk("weights_done")
        summed = by_chunk("summed")
        h_neigh_done = sem("h_neigh_done")
        sp_done = sem("sp_done")
        spT_ps = sem("spT_ps")
        spT_sb = sem("spT_sb")
        out_ps = sem("out_ps")
        y_done = sem("y_done")
        std_ready = sem("std_ready")
        rstd_ready = sem("rstd_ready")
        normed = sem("normed")
        stored = sem("stored")

        own = {name: sem(f"dve_{name}") for name in
               ("rel", "base", "scaled", "score", "s0", "r1", "s1", "r2", "nmax", "m0", "q1", "m1", "q2",
                "emax", "den", "rden", "z1", "z2", "y", "bn", "aggr")}

        block = ctx.enter_context(nc.Block())

        def pipeline(e, step):
            step(0, 0)
            step(1, 1)
            with e.Fori(1, BLOCKS // 2 - 1) as pair:
                for q in range(2):
                    step(pair * 2 + q, q)
            step(BLOCKS - 2, 0)
            step(BLOCKS - 1, 1)

        def known(b):
            return isinstance(b, int)

        def half(b, q):
            return b // 2 if known(b) else (b - q) // 2

        @block.sync
        def _(sp):
            sp.dma_start(rows_i[0:ROWS, :], dst.rearrange("(r c) -> r c", r=ROWS)).then_inc(rows_in, 16)
            sp.dma_start(watt_sb[:, :], watt).then_inc(w_in, 16)
            sp.dma_start(x_sb[:, 0:BLOCKS - 1, :],
                         x[0:(BLOCKS - 1) * P, :].rearrange("(b p) d -> p b d", p=P)).then_inc(x_in, 16)
            sp.dma_start(w12[:, 0, :], w1).then_inc(w_in, 16)
            sp.dma_start(w12[:, 1, :], w2).then_inc(w_in, 16)
            for tile, vector in ((batt_bc, batt), (b1_bc, b1), (b2_bc, b2)):
                sp.dma_start(tile[:, :], vector.rearrange("(a d) -> a d", a=1).to_broadcast([P, D]))\
                    .then_inc(w_in, 16)
            sp.wait_ge(pool_c, 1)
            sp.dma_start(x_sb[0:LAST_NODES, BLOCKS - 1, :], x[(BLOCKS - 1) * P:N, :]).then_inc(x_in, 16)
            with sp.Fori(0, STEPS - 1) as s:
                sp.wait_ge(h_sb, s + 1)
                sp.dma_start(table[bass.ds(s * (STEP * P), STEP * P), 0:D].rearrange("(b p) d -> p b d", p=P),
                             y_sb[:, bass.ds(s * STEP, STEP), :]).then_inc(h_out, 16)
            sp.wait_ge(h_sb, STEPS)
            at = (STEPS - 1) * STEP
            sp.dma_start(table[at * P:(BLOCKS - 1) * P, 0:D].rearrange("(b p) d -> p b d", p=P),
                         y_sb[:, at:BLOCKS - 1, :]).then_inc(h_out, 16)
            sp.dma_start(table[(BLOCKS - 1) * P:N, 0:D], y_sb[0:LAST_NODES, BLOCKS - 1, :]).then_inc(h_out, 16)

            sp.wait_ge(windows_ready, 1)

            def load(b, q):
                if not known(b) or b >= 2:
                    sp.wait_ge(scored[NC - 1], b - 1)
                o = sp.value_load(start_i[0:1, bass.ds(b, 1)] if not known(b) else start_i[0:1, b:b + 1],
                                  min_val=0, max_val=E - WINDOW)
                for tile, vector in ((src_i[q], src), (dst_i[q], dst)):
                    sp.dma_start(tile[:, 0:MAIN], vector[bass.ds(o, MAIN * P)].rearrange("(p g) -> p g", g=MAIN))\
                        .then_inc(loaded[q], 16)
                    sp.dma_start(tile[:, MAIN:TILES],
                                 vector[bass.ds(o + MAIN * P, TAIL * P)].rearrange("(g p) -> p g", p=P),
                                 allow_slow_non_contiguous=True)\
                        .then_inc(loaded[q], 16)
                sp.dma_start(edge[q][:, 0:MAIN, :],
                             edge_attr[bass.ds(o, MAIN * P), :].rearrange("(p g) d -> p g d", g=MAIN))\
                    .then_inc(loaded[q], 16)
                sp.dma_start(edge[q][:, MAIN:TILES, :],
                             edge_attr[bass.ds(o + MAIN * P, TAIL * P), :].rearrange("(g p) d -> p g d", p=P))\
                    .then_inc(loaded[q], 16)

            pipeline(sp, load)

            for n, (a, b) in enumerate(((0, BLOCKS // 2), (BLOCKS // 2, BLOCKS - 1))):
                sp.wait_ge(normed, b if b < BLOCKS - 1 else BLOCKS)
                sp.dma_start(out[a * P:b * P, :].rearrange("(b p) d -> p b d", p=P), y_sb[:, a:b, :])\
                    .then_inc(stored, 16)
            sp.dma_start(out[(BLOCKS - 1) * P:N, :], y_sb[0:LAST_NODES, BLOCKS - 1, :]).then_inc(stored, 16)
            sp.wait_ge(stored, 48)

        @block.gpsimd
        def _(pool):
            pool.memset(x_sb[:, BLOCKS - 1, :], 0.0).then_inc(pool_c, 1)
            pool.dma_start(table[:, D:2 * D], x).then_inc(x_copied, 16)
            pool.memset(ident[:, :], 0.0).then_inc(pool_c, 1)
            pool.wait_ge(pool_c, 2)
            pool.affine_select(out=ident[:, :], in_=ident[:, :], compare_op=ALU.not_equal, fill=1.0,
                               base=0, pattern=[[-1, P]], channel_multiplier=1).then_inc(pool_c, 1)
            pool.iota(iota_i[:, :], pattern=[[1, P]], base=0, channel_multiplier=0).then_inc(pool_c, 1)
            pool.iota(bound_i[:, :], pattern=[[0, 1]], base=0, channel_multiplier=P).then_inc(pool_c, 1)
            pool.iota(bound_row_i[:, :], pattern=[[P, P]], base=0, channel_multiplier=0).then_inc(pool_c, 1)
            pool.memset(sel[:, :, :], 1.0).then_inc(pool_c, 1)
            pool.wait_ge(pool_c, 7)
            pool.affine_select(out=sel[:, :, :], in_=sel[:, :, :], compare_op=ALU.is_ge, fill=0.0,
                               base=0, pattern=[[-3, TILES], [0, P]], channel_multiplier=1).then_inc(pool_c, 1)
            pool.wait_ge(pool_c, 8)
            pool.affine_select(out=sel[:, :, :], in_=sel[:, :, :], compare_op=ALU.is_ge, fill=0.0,
                               base=2, pattern=[[3, TILES], [0, P]], channel_multiplier=-1).then_inc(pool_c, 1)
            for q in range(2):
                pool.memset(got[q][:, MAIN:TILES, 0:2 * D], 0.0).then_inc(pool_c, 1)
            pool.wait_ge(pool_c, 11)

            pool.wait_ge(row_ready, 1)
            pool.indirect_dma_start(rows_i[0:BLOCKS + 1, :], None, dst.rearrange("(r c) -> r c", r=ROWS),
                                    bass.IndirectOffsetOnAxis(ap=row_idx[0:BLOCKS + 1, :], axis=0),
                                    bounds_check=ROWS - 1, oob_is_err=True).then_inc(rows_got, 16)

            pool.wait_ge(windows_ready, 1)
            pool.wait_ge(x_copied, 16)
            pool.wait_ge(h_out, 16 * (STEPS + 1))

            def gather(b, q):
                if not known(b) or b >= 2:
                    pool.wait_ge(summed[0], b - 1)
                pool.wait_ge(loaded[q], (half(b, q) + 1) * (16 * LOADS))
                n = pool.value_load(count_i[0:1, bass.ds(b, 1)] if not known(b) else count_i[0:1, b:b + 1],
                                    min_val=0, max_val=E)
                for c, tiles in enumerate(CHUNKS):
                    if c and (not known(b) or b >= 2):
                        pool.wait_ge(pool_c, 11)
                        pool.wait_ge(summed[c], b - 1)
                    for g in tiles:
                        def one():
                            pool.indirect_dma_start(got[q][:, g, 0:2 * D], None, table,
                                                    bass.IndirectOffsetOnAxis(ap=src_i[q][:, g:g + 1], axis=0),
                                                    bounds_check=N - 1, oob_is_err=True)\
                                .then_inc(gathered[q][c], 16)
                        if g <= MAIN:
                            one()
                        else:
                            with pool.If(n > g * P):
                                one()
                            with pool.Else():
                                pool.inc_swdge_sem([gathered[q][c]], [16], mode="add")

            pipeline(pool, gather)

        @block.scalar
        def _(act):
            act.wait_ge(wT_ps, 1)
            act.activation(wattT[:, :], ps_misc[0:D, 0:D], ACT.Copy).then_inc(w_ready, 1)
            act.activation(w12T[:, :], ps_acc[:, 0:D], ACT.Copy).then_inc(w_ready, 1)
            act.wait_ge(first_ps, 1)
            act.activation(first_row[0:1, :], ps_acc[0:1, 128:256], ACT.Copy).then_inc(first_ready, 1)
            with act.Fori(0, STEPS) as s:
                act.wait_ge(xT_ps, s + 1)
                act.activation(xT[:, 0:4, :], ps_hd[0][0:D, :].rearrange("p (b n) -> p b n", n=P), ACT.Copy)
                act.activation(xT[:, 4:STEP, :],
                               ps_hd[1][0:D, 0:(STEP - 4) * P].rearrange("p (b n) -> p b n", n=P),
                               ACT.Copy).then_inc(xT_sb, 1)

            def copy_mask(b, q):
                for c, tiles in enumerate(CHUNKS):
                    act.wait_ge(maskT_ps[c], b + 1)
                    a, z = tiles[0], tiles[-1] + 1
                    ps = ps_maskT[(q + c) % 2][:, 0:(z - a) * P].rearrange("p (g e) -> p g e", e=P)
                    act.activation(maskT[q][:, a:z, :], ps, ACT.Copy)
                    act.activation(hotT[q][:, a:z, :], ps, ACT.Copy, bias=1.0,
                                   scale=1.0 / MASKED).then_inc(maskT_sb[c], 1)

            def tanh(b, q, c):
                a, z = CHUNKS[c][0], CHUNKS[c][-1] + 1
                act.wait_ge(added[c], b + 1)
                act.activation(edge[q][:, a:z, :], edge[q][:, a:z, :], ACT.Tanh).then_inc(tanh_done[c], 1)

            def weigh(b, q, c):
                if c == 0:
                    act.wait_ge(arg_done, b + 1)
                if not known(b) or b >= 1:
                    act.wait_ge(summed[c], b)
                for g in CHUNKS[c]:
                    last = act.activation(weight[:, g, :], mask[q][:, g, :], ACT.Exp, bias=arg[:, g:g + 1])
                last.then_inc(weights_done[c], 1)

            def copy_scores(b):
                act.wait_ge(sT_ps, b + 1)
                act.activation(score3T[:, :], m_sT, ACT.Copy).then_inc(sT_sb, 1)

            def finish(b):
                act.wait_ge(spT_ps, b + 1)
                act.activation(sum_prodT[:, :], m_spT, ACT.Copy).then_inc(spT_sb, 1)

            copy_mask(0, 0)

            def step(b, q):
                lag = not known(b) or b >= 1
                if lag:
                    copy_scores(b - 1)
                tanh(b, q, 0)
                if lag:
                    weigh(b - 1, 1 - q, 0)
                    weigh(b - 1, 1 - q, 1)
                tanh(b, q, 1)
                if lag:
                    weigh(b - 1, 1 - q, 2)
                    weigh(b - 1, 1 - q, 3)
                tanh(b, q, 2)
                if lag:
                    weigh(b - 1, 1 - q, 4)
                tanh(b, q, 3)
                if not known(b) or b + 1 < BLOCKS:
                    copy_mask(b + 1, 1 - q)
                if lag:
                    finish(b - 1)
                tanh(b, q, 4)

            pipeline(act, step)
            copy_scores(BLOCKS - 1)
            for c in range(NC):
                weigh(BLOCKS - 1, 1, c)
            finish(BLOCKS - 1)
            act.wait_ge(y_done, BLOCKS)
            act.activation(std[:, :], stats[:, :, 1], ACT.Sqrt, bias=eps_col[:, 0:1]).then_inc(std_ready, 1)

        @block.tensor
        def _(pe):
            pe.wait_ge(pool_c, 3)
            pe.wait_ge(w_in, 16 * 6)
            pe.transpose(ps_misc[0:D, 0:D], watt_sb[:, :], ident[0:D, 0:D])
            pe.transpose(ps_acc[:, 0:D], w12[:, :, :].rearrange("o a i -> o (a i)"),
                         ident[0:D, 0:D]).then_inc(wT_ps, 1)
            pe.wait_ge(rows_counted, 1)
            pe.matmul(ps_sc[0][0:BLOCKS + 1, 0:1], below_row[0:ROWS, 0:BLOCKS + 1], ones[0:ROWS, :],
                      start=True, stop=True).then_inc(below_ready, 1)
            pe.wait_ge(first_ready, 1)
            pe.wait_ge(w_ready, 2)
            pe.transpose(ps_acc[0:1, 128:256], first[:, :], ident[:, :]).then_inc(first_ps, 1)

            pe.wait_ge(x_in, 32)

            def transpose_x(s):
                if s >= 1:
                    pe.wait_ge(xT_sb, s)
                for k in range(STEP):
                    last = pe.transpose(ps_hd[k // 4][0:D, (k % 4) * P:(k % 4 + 1) * P],
                                        x_sb[:, s * STEP + k, :], ident[:, :])
                last.then_inc(xT_ps, 1)

            def project(s):
                pe.wait_ge(xT_sb, s + 1)
                if s >= 1:
                    pe.wait_ge(h_sb, s)
                for k in range(STEP):
                    last = pe.matmul(ps_sc[1][:, k * D:(k + 1) * D], xT[:, k, :], wattT[:, :],
                                     start=True, stop=True)
                last.then_inc(h_ps, 1)

            for s in range(STEPS):
                transpose_x(s)
                project(s)

            def transpose_mask(b, q):
                for c, tiles in enumerate(CHUNKS):
                    pe.wait_ge(mask_built[c], b + 1)
                    if c >= 2 or not known(b) or b >= 1:
                        pe.wait_ge(maskT_sb[(c - 2) % NC], b + 1 if c >= 2 else b)
                    for k, g in enumerate(tiles):
                        last = pe.transpose(ps_maskT[(q + c) % 2][:, k * P:(k + 1) * P], mask[q][:, g, :],
                                            ident16[:, :])
                    last.then_inc(maskT_ps[c], 1)

            def expand(b, q, c):
                if c == 0:
                    pe.wait_ge(maskT_sb[NC - 1], b + 1)
                if c >= 2 or not known(b) or b >= 1:
                    pe.wait_ge(hd_used[(c - 2) % NC], b + 1 if c >= 2 else b)
                for k, g in enumerate(CHUNKS[c]):
                    for part in range(3):
                        rhs = h3[:, b, part, :] if known(b) else \
                            h3[:, bass.ds(b, 1), part, :].rearrange("p a d -> p (a d)")
                        last = pe.matmul(ps_hd[(q + c) % 2][:, k * D:(k + 1) * D], hotT[q][:, g, :], rhs,
                                         start=(part == 0), stop=(part == 2))
                last.then_inc(hd_ready[c], 1)

            def transpose_scores(b):
                pe.wait_ge(pool_c, 11)
                pe.wait_ge(split_done, b + 1)
                pe.transpose(m_sT, score3[:, :, :].rearrange("p g s -> p (g s)"), ident16[:, :]).then_inc(sT_ps, 1)

            def spread_scores(b, q):
                pe.wait_ge(sT_sb, b + 1)
                for c, tiles in enumerate(CHUNKS):
                    if c >= 2 or not known(b) or b >= 1:
                        pe.wait_ge(sc_used[(c - 2) % NC], b + 1 if c >= 2 else b)
                    for k, g in enumerate(tiles):
                        last = pe.matmul(ps_sc[(q + c) % 2][:, k * P:(k + 1) * P], sel[:, g, :], score3T[:, :],
                                         start=True, stop=True)
                    last.then_inc(sc_ready[c], 1)

            def spread_max(b, q):
                pe.wait_ge(max_split, b + 1)
                for g in range(TILES):
                    last = pe.matmul(m_max[:, 3 * g:3 * g + 3], hotT[q][:, g, :], max3[:, :],
                                     start=True, stop=True)
                last.then_inc(max_ps, 1)

            def sum_edges(b, q, c):
                if c == 0 and (not known(b) or b >= 1):
                    pe.wait_ge(h_neigh_done, b)
                pe.wait_ge(weights_done[c], b + 1)
                for g in CHUNKS[c]:
                    last = pe.matmul(ps_acc[:, 0:D + 1], weight[:, g, :], got[q][:, g, D:2 * D + 1],
                                     start=(g == 0), stop=(g == TILES - 1))
                last.then_inc(summed[c], 1)

            def finish(b):
                pe.wait_ge(sp_done, b + 1)
                pe.transpose(m_spT, sum_prod[:, :], ident[:, :]).then_inc(spT_ps, 1)
                pe.wait_ge(spT_sb, b + 1)
                pe.matmul(m_out, sum_prodT[:, :], w12T[:, :], start=True, stop=True).then_inc(out_ps, 1)

            transpose_mask(0, 0)
            pe.wait_ge(h3_ready, 1)

            def step(b, q):
                lag = not known(b) or b >= 1
                expand(b, q, 0)
                if lag:
                    transpose_scores(b - 1)
                    spread_scores(b - 1, 1 - q)
                    spread_max(b - 1, 1 - q)
                expand(b, q, 1)
                if lag:
                    sum_edges(b - 1, 1 - q, 0)
                    sum_edges(b - 1, 1 - q, 1)
                expand(b, q, 2)
                if lag:
                    sum_edges(b - 1, 1 - q, 2)
                    sum_edges(b - 1, 1 - q, 3)
                expand(b, q, 3)
                if lag:
                    sum_edges(b - 1, 1 - q, 4)
                if not known(b) or b + 1 < BLOCKS:
                    transpose_mask(b + 1, 1 - q)
                if lag:
                    finish(b - 1)
                expand(b, q, 4)

            pipeline(pe, step)
            b = BLOCKS - 1
            transpose_scores(b)
            spread_scores(b, 1)
            spread_max(b, 1)
            for c in range(NC):
                sum_edges(b, 1, c)
            finish(b)

        @block.vector
        def _(dve):
            done = [0]

            def link(ins):
                done[0] += 1
                ins.then_inc(dve_c, 1)
                dve.wait_ge(dve_c, done[0])

            dve.memset(ones[:, :], 1.0)
            dve.memset(got[0][:, :, 2 * D:2 * D + 1], 1.0)
            dve.memset(got[1][:, :, 2 * D:2 * D + 1], 1.0)
            dve.memset(eps_col[:, :], EPS_NORM)
            dve.memset(first[:, :], 0.0)
            link(dve.memset(base[:, :], 0.0))
            dve.wait_ge(pool_c, 11)
            dve.tensor_copy(ident16[:, :], ident[:, :])
            dve.tensor_copy(iota_h[:, :], iota_i[:, :])
            dve.tensor_copy(bound[:, :], bound_i[:, :])
            link(dve.tensor_copy(bound_row[:, :], bound_row_i[:, :]))
            dve.wait_ge(rows_in, 16)
            link(dve.tensor_copy(row_last[0:ROWS, :], rows_i[0:ROWS, SEARCH_ROW - 1:SEARCH_ROW]))
            dve.tensor_scalar(below_row[0:ROWS, :], bound_row[0:ROWS, :], row_last[0:ROWS, 0:1], None,
                              ALU.is_gt).then_inc(rows_counted, 1)
            dve.wait_ge(below_ready, 1)
            B1 = BLOCKS + 1
            link(dve.tensor_scalar(row_f[0:B1, :], ps_sc[0][0:B1, 0:1], float(ROWS - 1), None, ALU.min))
            dve.tensor_copy(row_idx[0:B1, :], row_f[0:B1, :]).then_inc(row_ready, 1)
            dve.wait_ge(rows_got, 16)
            link(dve.tensor_scalar(below[0:B1, :], rows_i[0:B1, :], bound[0:B1, 0:1], None, ALU.is_lt))
            link(dve.tensor_reduce(below_n[0:B1, :], below[0:B1, :], AX.X, ALU.add))
            dve.scalar_tensor_tensor(out=first[0:B1, :], in0=row_f[0:B1, :], scalar=float(SEARCH_ROW),
                                     in1=below_n[0:B1, :], op0=ALU.mult, op1=ALU.add).then_inc(first_ready, 1)
            dve.wait_ge(first_ready, 2)
            link(dve.tensor_scalar(start_row[:, :], first_row[:, :], float(E - WINDOW), None, ALU.min))
            link(dve.tensor_tensor(count_row[:, 0:BLOCKS], first_row[:, 1:B1], start_row[:, 0:BLOCKS],
                                   ALU.subtract))
            link(dve.tensor_copy(start_i[:, 0:BLOCKS], start_row[:, 0:BLOCKS]))
            dve.tensor_copy(count_i[:, 0:BLOCKS], count_row[:, 0:BLOCKS]).then_inc(windows_ready, 1)
            dve.wait_ge(w_in, 16 * 6)
            link(dve.tensor_tensor(b12[:, :], b1_bc[:, :], b2_bc[:, :], ALU.add))
            with dve.Fori(0, STEPS) as s:
                dve.wait_ge(h_ps, s + 1)
                dve.tensor_tensor(y_sb[:, bass.ds(s * STEP, STEP), :],
                                  ps_sc[1][:, 0:STEP * D].rearrange("p (b d) -> p b d", d=D),
                                  batt_bc[:, :].rearrange("p (a d) -> p a d", a=1).to_broadcast([P, STEP, D]),
                                  ALU.add).then_inc(h_sb, 1)
            dve.wait_ge(h_sb, STEPS)
            dve.wait_ge(h_out, 16 * (STEPS + 1))
            link(dve.tensor_copy(h3[:, :, 0, :], y_sb[:, :, :]))
            link(dve.tensor_tensor(y_sb[:, :, :], y_sb[:, :, :], h3[:, :, 0, :], ALU.subtract))
            link(dve.tensor_copy(h3[:, :, 1, :], y_sb[:, :, :]))
            link(dve.tensor_tensor(y_sb[:, :, :], y_sb[:, :, :], h3[:, :, 1, :], ALU.subtract))
            dve.tensor_copy(h3[:, :, 2, :], y_sb[:, :, :]).then_inc(h3_ready, 1)
            dve.wait_ge(h3_ready, 1)

            def chain(name, ins, count):
                ins.then_inc(own[name], 1)
                dve.wait_ge(own[name], count + 1)

            def build_mask(b, q):
                dve.wait_ge(loaded[q], (half(b, q) + 1) * (16 * LOADS))
                if not known(b) or b >= 2:
                    dve.wait_ge(weights_done[NC - 1], b - 1)
                chain("rel", dve.tensor_scalar(dst_rel[q][:, :], dst_i[q][:, :], base[:, 0:1], None,
                                               ALU.subtract), b)
                chain("base", dve.tensor_scalar(base[:, :], base[:, :], float(P), None, ALU.add), b)
                for c, tiles in enumerate(CHUNKS):
                    for g in tiles:
                        last = dve.tensor_scalar(mask[q][:, g, :], iota_h[:, :], dst_rel[q][:, g:g + 1],
                                                 -MASKED, ALU.not_equal, ALU.mult)
                    last.then_inc(mask_built[c], 1)

            def add(b, q, c):
                a, z = CHUNKS[c][0], CHUNKS[c][-1] + 1
                dve.wait_ge(gathered[q][c], (half(b, q) + 1) * (16 * (z - a)))
                dve.tensor_tensor(edge[q][:, a:z, :], edge[q][:, a:z, :], got[q][:, a:z, 0:D],
                                  ALU.add).then_inc(added[c], 1)

            def dot(b, q, c):
                a, z = CHUNKS[c][0], CHUNKS[c][-1] + 1
                dve.wait_ge(tanh_done[c], b + 1)
                dve.wait_ge(hd_ready[c], b + 1)
                ps = ps_hd[(q + c) % 2][:, 0:(z - a) * D].rearrange("p (g d) -> p g d", d=D)
                dve.tensor_tensor(edge[q][:, a:z, :], edge[q][:, a:z, :], ps, ALU.mult).then_inc(hd_used[c], 1)
                dve.wait_ge(hd_used[c], b + 1)
                dve.tensor_reduce(raw[q][:, a:z], edge[q][:, a:z, :], AX.X, ALU.add).then_inc(scored[c], 1)

            def scale_scores(b, q):
                dve.wait_ge(scored[NC - 1], b + 1)
                chain("scaled", dve.tensor_scalar(scaled[:, :], raw[q][:, :], D ** -0.5, None, ALU.mult), b)
                chain("score", dve.scalar_tensor_tensor(out=score[:, :], in0=scaled[:, :], scalar=SLOPE,
                                                        in1=scaled[:, :], op0=ALU.mult, op1=ALU.max), b)
                chain("s0", dve.tensor_copy(score3[:, :, 0], score[:, :]), b)
                chain("r1", dve.tensor_tensor(rest1[:, :], score[:, :], score3[:, :, 0], ALU.subtract), b)
                chain("s1", dve.tensor_copy(score3[:, :, 1], rest1[:, :]), b)
                chain("r2", dve.tensor_tensor(rest2[:, :], rest1[:, :], score3[:, :, 1], ALU.subtract), b)
                dve.tensor_copy(score3[:, :, 2], rest2[:, :]).then_inc(split_done, 1)

            def take_max(b, q):
                for c, tiles in enumerate(CHUNKS):
                    n = len(tiles) * P
                    dve.wait_ge(pool_c, 11)
                    dve.wait_ge(sc_ready[c], b + 1)
                    m = maskT[q][:, tiles[0]:tiles[-1] + 1, :].rearrange("p g e -> p (g e)")
                    dve.tensor_tensor_reduce(
                        out=m, in0=ps_sc[(q + c) % 2][:, 0:n], in1=m,
                        scale=1.0, scalar=LOWEST, op0=ALU.add, op1=ALU.max,
                        accum_out=chunk_max[:, c:c + 1]).then_inc(sc_used[c], 1)
                dve.wait_ge(sc_used[NC - 1], b + 1)
                chain("nmax", dve.tensor_reduce(node_max[:, :], chunk_max[:, :], AX.X, ALU.max), b)
                chain("m0", dve.tensor_copy(max3[:, 0:1], node_max[:, :]), b)
                chain("q1", dve.tensor_tensor(mrest1[:, :], node_max[:, :], max3[:, 0:1], ALU.subtract), b)
                chain("m1", dve.tensor_copy(max3[:, 1:2], mrest1[:, :]), b)
                chain("q2", dve.tensor_tensor(mrest2[:, :], mrest1[:, :], max3[:, 1:2], ALU.subtract), b)
                dve.tensor_copy(max3[:, 2:3], mrest2[:, :]).then_inc(max_split, 1)

            def exponents(b):
                dve.wait_ge(max_ps, b + 1)
                chain("emax", dve.tensor_reduce(edge_max[:, :], m_max.rearrange("p (g s) -> p g s", s=3),
                                                AX.X, ALU.add), b)
                dve.tensor_tensor(arg[:, :], score[:, :], edge_max[:, :], ALU.subtract).then_inc(arg_done, 1)

            def at(t, b):
                return t[:, b, :] if known(b) else t[:, bass.ds(b, 1), :].rearrange("p a d -> p (a d)")

            def neighbours(b):
                dve.wait_ge(summed[NC - 1], b + 1)
                chain("den", dve.tensor_scalar(den[:, :], ps_acc[:, D:D + 1], EPS_ALPHA, None, ALU.add), b)
                chain("rden", dve.reciprocal(rden[:, :], den[:, :]), b)
                dve.tensor_scalar(h_neigh[:, :], ps_acc[:, 0:D], rden[:, 0:1], None, ALU.mult)\
                    .then_inc(h_neigh_done, 1)
                dve.wait_ge(h_neigh_done, b + 1)
                dve.tensor_tensor(sum_prod[:, 0:D], h_neigh[:, :], at(x_sb, b), ALU.add)
                dve.tensor_tensor(sum_prod[:, D:2 * D], h_neigh[:, :], at(x_sb, b), ALU.mult).then_inc(sp_done, 1)

            def residual(b):
                dve.wait_ge(out_ps, b + 1)
                chain("z1", dve.tensor_tensor(z1[:, :], m_out, b12[:, :], ALU.add), b)
                chain("z2", dve.scalar_tensor_tensor(out=z2[:, :], in0=z1[:, :], scalar=SLOPE, in1=z1[:, :],
                                                     op0=ALU.mult, op1=ALU.max), b)
                chain("y", dve.tensor_tensor(y_new[:, :], at(x_sb, b), z2[:, :], ALU.add), b)
                dve.tensor_copy(at(y_sb, b), y_new[:, :])
                dve.bn_stats(bn6[:, :], y_new[:, :]).then_inc(own["bn"], 1)
                dve.wait_ge(pool_c, 11)
                dve.wait_ge(own["bn"], b + 1)
                chain("aggr", dve.bn_aggr(mean_var[:, :], bn6[:, :]), b)
                dve.tensor_copy(at(stats, b), mean_var[:, :]).then_inc(y_done, 1)

            build_mask(0, 0)

            def step(b, q):
                lag = not known(b) or b >= 1
                if lag:
                    scale_scores(b - 1, 1 - q)
                add(b, q, 0)
                if lag:
                    take_max(b - 1, 1 - q)
                dot(b, q, 0)
                if lag:
                    exponents(b - 1)
                for c in (1, 2, 3):
                    add(b, q, c)
                    dot(b, q, c)
                if not known(b) or b + 1 < BLOCKS:
                    build_mask(b + 1, 1 - q)
                if lag:
                    neighbours(b - 1)
                add(b, q, 4)
                if lag:
                    residual(b - 1)
                dot(b, q, 4)

            pipeline(dve, step)
            b = BLOCKS - 1
            scale_scores(b, 1)
            take_max(b, 1)
            exponents(b)
            neighbours(b)
            residual(b)
            dve.wait_ge(std_ready, 1)
            dve.reciprocal(rstd[:, :], std[:, :]).then_inc(rstd_ready, 1)
            dve.wait_ge(rstd_ready, 1)
            with dve.Fori(0, BLOCKS) as b:
                y = at(y_sb, b)
                dve.tensor_scalar(y, y, stats[:, bass.ds(b, 1), 0:1].rearrange("p a s -> p (a s)"),
                                  rstd[:, bass.ds(b, 1)], ALU.subtract, ALU.mult).then_inc(normed, 1)


_INS = ['x', 'src', 'dst', 'edge_attr_64', 'L0_gnn_W1_w', 'L0_gnn_W1_b', 'L0_gnn_W2_w', 'L0_gnn_W2_b',
        'L0_gnn_Watt_w', 'L0_gnn_Watt_b']


def kernel(**inputs):
    import numpy as _np
    import concourse.bacc as _bacc
    from concourse.bass_utils import run_bass_kernel_spmd as _run

    nc = _bacc.Bacc("TRN2", target_bir_lowering=False, num_devices=1)
    arrays, args = {}, []
    for name in _INS:
        a = _np.ascontiguousarray(inputs[name])
        arrays[f"in_{name}"] = a
        args.append(nc.dram_tensor(f"in_{name}", a.shape, mybir.dt.from_np(a.dtype), kind="ExternalInput").ap())
    args.append(nc.dram_tensor("out_0", arrays["in_x"].shape, F32, kind="ExternalOutput").ap())
    gnn_layer(nc, *args)
    r = _run(nc, [arrays], core_ids=[0])
    return r.results[0]["out_0"]
```

```python
from collections import namedtuple
from contextlib import ExitStack

import concourse.bass as bass
from concourse import mybir

ALU = mybir.AluOpType
ACT = mybir.ActivationFunctionType
AX = mybir.AxisListType
F32 = mybir.dt.float32
BF16 = mybir.dt.bfloat16
I32 = mybir.dt.int32

P = 128
MAIN = 16
TAIL = 3
TILES = MAIN + TAIL
CHUNK = 4
BUFS = 4
SEARCH_ROW = 1700
STEP = 8
PIECES = 4
MASKED = float(2 ** 100)
LOWEST = -3.0e38
SLOPE = 0.2
EPS_ALPHA = 1e-9
EPS_NORM = 1e-5

Block = namedtuple("Block", "n four two fours twos known")


def at_block(turn, k):
    return Block(turn * BUFS + k, k % BUFS, k % 2, turn + k // BUFS, turn * 2 + k // 2, isinstance(turn, int))


def gnn_layer(nc, x, src, dst, edge_attr, w1, b1, w2, b2, watt, batt, out):
    N, D = x.shape
    E, = src.shape
    BLOCKS = (N + P - 1) // P
    LAST = BLOCKS - 1
    LAST_NODES = N - LAST * P
    WINDOW = TILES * P
    ROWS = E // SEARCH_ROW
    CHUNKS = [range(a, min(a + CHUNK, TILES)) for a in range(0, TILES, CHUNK)]
    NC = len(CHUNKS)
    STEPS = [range(a, min(a + STEP, BLOCKS)) for a in range(0, BLOCKS, STEP)]
    PIECE = STEP * (len(STEPS) // PIECES)
    TURNS = (BLOCKS - 2) // BUFS
    EARLY = BLOCKS - 3
    NORMED = [(0, EARLY // 3), (EARLY // 3, 2 * EARLY // 3), (2 * EARLY // 3, EARLY), (EARLY, BLOCKS)]
    SCALE = D ** -0.5
    assert D == 64 and ROWS * SEARCH_ROW == E and TURNS * BUFS + 2 == BLOCKS and BLOCKS % 2 == 0
    assert (BLOCKS - (PIECES - 1) * PIECE) * D <= MAIN * (2 * D + 1) and BUFS == PIECES
    assert BLOCKS + 1 <= P and ROWS <= P and WINDOW <= E and LAST_NODES > 0

    with ExitStack() as ctx:
        def sb(name, shape, dt=F32):
            return ctx.enter_context(nc.sbuf_tensor(name, shape, dt))

        def bank(name, dt=F32):
            return ctx.enter_context(nc.psum_tensor(name, [P, 512 * 4 // mybir.dt.size(dt)], dt))

        def sem(name):
            return ctx.enter_context(nc.semaphore(name))

        def by_chunk(name):
            return [sem(f"{name}_{c}") for c in range(NC)]

        table = nc.dram_tensor("table", (N, 2 * D), F32, kind="Internal").ap()

        hx = sb("hx", [P, BLOCKS, 2 * D])
        h3 = sb("h3", [P, BLOCKS, 3, D], BF16)
        stats = sb("stats", [P, BLOCKS, 2])
        std = sb("std", [P, BLOCKS])
        rstd = sb("rstd", [P, BLOCKS])
        ident = sb("ident", [P, P])
        ident16 = sb("ident16", [P, P], BF16)
        mask16 = sb("mask16", [P, P], BF16)
        iota_h = sb("iota_h", [P, P], BF16)
        iota_i = sb("iota_i", [P, P], I32)
        sel = sb("sel", [3 * TILES, TILES, P], BF16)
        watt2 = sb("watt2", [P, P])
        watt2T = sb("watt2T", [P, P])
        w12 = sb("w12", [D, 2, D])
        w12T = sb("w12T", [P, D])
        batt_bc = sb("batt_bc", [P, D])
        b1_bc = sb("b1_bc", [P, D])
        b2_bc = sb("b2_bc", [P, D])
        b12 = sb("b12", [P, D])
        eps_col = sb("eps_col", [P, 1])
        ones = sb("ones", [P, 1])

        bound_i = sb("bound_i", [P, 1], I32)
        bound = sb("bound", [P, 1])
        bound_row_i = sb("bound_row_i", [P, P], I32)
        bound_row = sb("bound_row", [P, P])
        row_last = sb("row_last", [P, 1])
        below_row = sb("below_row", [P, P])
        row_f = sb("row_f", [P, 1])
        row_idx = sb("row_idx", [P, 1], I32)
        below_n = sb("below_n", [P, 1])
        first = sb("first", [P, 1])
        first_row = sb("first_row", [1, P])
        start_row = sb("start_row", [1, P])
        count_row = sb("count_row", [1, P])
        start_i = sb("start_i", [1, P], I32)
        count_i = sb("count_i", [1, P], I32)

        src_i = [sb(f"src_i{k}", [P, TILES], I32) for k in range(BUFS)]
        dst_i = [sb(f"dst_i{k}", [P, TILES], I32) for k in range(BUFS)]
        edge = [sb(f"edge{k}", [P, TILES, D]) for k in range(2)]
        got = [sb(f"got{k}", [P, TILES, 2 * D + 1]) for k in range(BUFS)]
        other = [sb(f"other{k}", [P, TILES, P], BF16) for k in range(BUFS)]
        hotT = [sb(f"hotT{k}", [P, TILES, P], BF16) for k in range(BUFS)]
        raw = [sb(f"raw{k}", [P, TILES]) for k in range(2)]
        arg = [sb(f"arg{k}", [P, TILES]) for k in range(2)]
        base = sb("base", [P, 1])
        dst_rel = sb("dst_rel", [P, TILES, 2], BF16)
        product = sb("product", [P, D])
        score = sb("score", [P, TILES])
        score3 = sb("score3", [P, TILES, 3], BF16)
        rest1 = sb("rest1", [P, TILES])
        rest2 = sb("rest2", [P, TILES])
        score3T = sb("score3T", [3 * TILES, P], BF16)
        chunk_max = sb("chunk_max", [P, NC])
        node_max = sb("node_max", [P, 1])
        max3 = sb("max3", [P, 3], BF16)
        mrest1 = sb("mrest1", [P, 1])
        mrest2 = sb("mrest2", [P, 1])
        edge_max = sb("edge_max", [P, TILES])
        weight = sb("weight", [P, TILES, P])
        den = sb("den", [P, 1])
        rden = sb("rden", [P, 1])
        h_neigh = sb("h_neigh", [P, D])
        sum_prod = sb("sum_prod", [P, 2 * D])
        sum_prodT = sb("sum_prodT", [P, P])
        z1 = sb("z1", [P, D])
        z2 = sb("z2", [P, D])
        y_new = sb("y_new", [P, D])
        bn6 = sb("bn6", [P, 6])
        mean_var = sb("mean_var", [P, 2])
        rows_i = weight[:, :, :].rearrange("p g n -> p (g n)")[:, 0:SEARCH_ROW].bitcast(I32)
        below = hotT[1][:, :, :].rearrange("p g n -> p (g n)")[:, 0:SEARCH_ROW]
        xT = [edge[k][:, 0:STEP, :].rearrange("p g d -> p (g d)") for k in range(2)]
        x_piece = [t[:, :, :].rearrange("p g c -> p (g c)")[:, 0:(BLOCKS - (PIECES - 1) * PIECE) * D]
                   .rearrange("p (b d) -> p b d", d=D) for t in got]
        hrest = [other[2 + k][:, 0:8, :].rearrange("p g n -> p (g n)").bitcast(F32) for k in range(2)]

        ps_hd = [bank(f"ps_hd{k}") for k in range(2)]
        ps_other = [bank(f"ps_other{k}", BF16) for k in range(2)]
        ps_sc = [bank(f"ps_sc{k}") for k in range(2)]
        ps_acc = bank("ps_acc")
        ps_misc = bank("ps_misc")
        a_sum = ps_acc[:, 0:D + 1]
        a_out = ps_acc[:, 128:128 + D]
        a_sT = ps_acc[0:3 * TILES, 256:256 + P // 2].bitcast(BF16)
        m_max = ps_misc[:, 0:3 * TILES]
        m_spT = ps_misc[:, 128:256]

        consts = sem("consts")
        x_in = [sem(f"x_in{k}") for k in range(PIECES)]
        x_set = sem("x_set")
        ones_set = sem("ones_set")
        watt_in = sem("watt_in")
        w12_in = sem("w12_in")
        bias_in = sem("bias_in")
        rows_in = sem("rows_in")
        dve_c = sem("dve_c")
        w_ps = sem("w_ps")
        w_sb = sem("w_sb")
        rows_counted = sem("rows_counted")
        row_ps = sem("row_ps")
        row_ready = sem("row_ready")
        rows_got = sem("rows_got")
        first_ready = sem("first_ready")
        first_ps = sem("first_ps")
        first_sb = sem("first_sb")
        windows_ready = sem("windows_ready")
        xT_ps = sem("xT_ps")
        xT_sb = sem("xT_sb")
        h_ps = sem("h_ps")
        h_sb = sem("h_sb")
        table_out = sem("table_out")
        h3_ready = sem("h3_ready")
        index_in = [sem(f"index_in{k}") for k in range(BUFS)]
        edge_in = [sem(f"edge_in{k}") for k in range(2)]
        gathered = [[sem(f"gathered{k}_{c}") for c in range(NC)] for k in range(BUFS)]
        other_built = sem("other_built")
        other_ps = by_chunk("other_ps")
        hot_sb = by_chunk("hot_sb")
        hd_ready = by_chunk("hd_ready")
        added = by_chunk("added")
        tanh_done = by_chunk("tanh_done")
        scored = by_chunk("scored")
        split_done = sem("split_done")
        sT_ps = sem("sT_ps")
        sT_sb = sem("sT_sb")
        sc_ready = by_chunk("sc_ready")
        sc_used = by_chunk("sc_used")
        max_split = sem("max_split")
        max_ps = sem("max_ps")
        arg_done = sem("arg_done")
        weights_done = by_chunk("weights_done")
        summed = by_chunk("summed")
        h_neigh_done = sem("h_neigh_done")
        sp_done = sem("sp_done")
        spT_ps = sem("spT_ps")
        spT_sb = sem("spT_sb")
        out_ps = sem("out_ps")
        y_done = sem("y_done")
        own = {name: sem(f"dve_{name}") for name in
               ("rel", "base", "score", "s0", "r1", "s1", "r2", "nmax", "m0", "q1", "m1", "q2",
                "emax", "den", "rden", "z1", "z2", "y", "bn", "aggr")}
        std_ready = sem("std_ready")
        rstd_ready = sem("rstd_ready")
        centred = sem("centred")
        normed = sem("normed")
        stored = sem("stored")

        block = ctx.enter_context(nc.Block())

        def pipeline(e, step):
            def turn(t, k):
                step(*(at_block(t, k + j) for j in (-3, -2, -1, 0, 1, 2)))

            for k in range(BUFS):
                turn(0, k)
            with e.Fori(1, TURNS) as t:
                for k in range(BUFS):
                    turn(t, k)
            for k in range(TURNS * BUFS, BLOCKS):
                turn(0, k)

        def exists(b):
            return not b.known or 0 <= b.n < BLOCKS

        def follows(b, n):
            return not b.known or b.n >= n

        def cols(c):
            return CHUNKS[c][0], CHUNKS[c][-1] + 1

        def node_rows(t, b, a, z):
            if b.known:
                return t[:, b.n, a:z]
            return t[:, bass.ds(b.n, 1), a:z].rearrange("p a d -> p (a d)")

        @block.sync
        def _(sp):
            def load_x(k):
                a, z = k * PIECE, (k + 1) * PIECE if k < PIECES - 1 else LAST
                sp.dma_start(x_piece[k][:, 0:z - a, :], x[a * P:z * P, :].rearrange("(b p) d -> p b d", p=P))\
                    .then_inc(x_in[k], 16)

            load_x(0)
            sp.wait_ge(consts, 2)
            for k in range(2):
                sp.dma_start(watt2[k * D:(k + 1) * D, k * D:(k + 1) * D], watt).then_inc(watt_in, 16)
            sp.dma_start(batt_bc[:, :], batt.rearrange("(a d) -> a d", a=1).to_broadcast([P, D]))\
                .then_inc(bias_in, 16)
            sp.dma_start(rows_i[0:ROWS, :], dst.rearrange("(r c) -> r c", r=ROWS)).then_inc(rows_in, 16)
            for k in range(1, PIECES):
                load_x(k)
            sp.dma_start(x_piece[PIECES - 1][0:LAST_NODES, LAST - (PIECES - 1) * PIECE, :], x[LAST * P:N, :]).then_inc(x_in[PIECES - 1], 16)
            sp.dma_start(w12[:, 0, :], w1).then_inc(w12_in, 16)
            sp.dma_start(w12[:, 1, :], w2).then_inc(w12_in, 16)
            for tile, vector in ((b1_bc, b1), (b2_bc, b2)):
                sp.dma_start(tile[:, :], vector.rearrange("(a d) -> a d", a=1).to_broadcast([P, D]))\
                    .then_inc(bias_in, 16)
            for s, blocks in enumerate(STEPS):
                sp.wait_ge(x_set, min(s // (PIECE // STEP), PIECES - 1) + 1)
                sp.wait_ge(h_sb, s + 1)
                a, z = blocks[0], min(blocks[-1] + 1, LAST)
                sp.dma_start(table[a * P:z * P, :].rearrange("(b p) d -> p b d", p=P), hx[:, a:z, :])\
                    .then_inc(table_out, 16)
            sp.dma_start(table[LAST * P:N, :], hx[0:LAST_NODES, LAST, :]).then_inc(table_out, 16)

            sp.wait_ge(windows_ready, 1)

            def first_edge(b):
                return sp.value_load(start_i[0:1, b.n:b.n + 1] if b.known else start_i[0:1, bass.ds(b.n, 1)],
                                     min_val=0, max_val=E - WINDOW)

            def load_indices(b, o):
                for tile, vector in ((src_i[b.four], src), (dst_i[b.four], dst)):
                    sp.dma_start(tile[:, 0:MAIN], vector[bass.ds(o, MAIN * P)].rearrange("(p g) -> p g", g=MAIN))\
                        .then_inc(index_in[b.four], 16)
                    sp.dma_start(tile[:, MAIN:TILES],
                                 vector[bass.ds(o + MAIN * P, TAIL * P)].rearrange("(g p) -> p g", p=P),
                                 allow_slow_non_contiguous=True).then_inc(index_in[b.four], 16)

            def load_edges(b, o):
                sp.dma_start(edge[b.two][:, 0:MAIN, :],
                             edge_attr[bass.ds(o, MAIN * P), :].rearrange("(p g) d -> p g d", g=MAIN))\
                    .then_inc(edge_in[b.two], 16)
                sp.dma_start(edge[b.two][:, MAIN:TILES, :],
                             edge_attr[bass.ds(o + MAIN * P, TAIL * P), :].rearrange("(g p) d -> p g d", p=P))\
                    .then_inc(edge_in[b.two], 16)

            for n in range(2):
                load_indices(at_block(0, n), first_edge(at_block(0, n)))

            def step(third, before, prev, b, nxt, ahead):
                edges_at = first_edge(b)
                indices_at = first_edge(ahead) if exists(ahead) else None
                if follows(b, 2):
                    sp.wait_ge(scored[NC - 1], b.n - 1)
                load_edges(b, edges_at)
                if exists(ahead):
                    load_indices(ahead, indices_at)

            pipeline(sp, step)

            for k, (a, z) in enumerate(NORMED):
                sp.wait_ge(normed, k + 1)
                sp.dma_start(out[a * P:min(z, LAST) * P, :].rearrange("(b p) d -> p b d", p=P),
                             hx[:, a:min(z, LAST), 0:D]).then_inc(stored, 16)
            sp.dma_start(out[LAST * P:N, :], hx[0:LAST_NODES, LAST, 0:D]).then_inc(stored, 16)
            sp.wait_ge(stored, 16 * (len(NORMED) + 1))

        @block.gpsimd
        def _(pool):
            pool.memset(watt2[:, :], 0.0).then_inc(consts, 1)
            pool.memset(x_piece[PIECES - 1][:, LAST - (PIECES - 1) * PIECE, :], 0.0).then_inc(consts, 1)
            pool.iota(bound_row_i[:, :], pattern=[[P, P]], base=0, channel_multiplier=0).then_inc(consts, 1)
            pool.iota(bound_i[:, :], pattern=[[0, 1]], base=0, channel_multiplier=P).then_inc(consts, 1)
            pool.memset(ident[:, :], 0.0).then_inc(consts, 1)
            pool.wait_ge(consts, 5)
            pool.affine_select(out=ident[:, :], in_=ident[:, :], compare_op=ALU.not_equal, fill=1.0,
                               base=0, pattern=[[-1, P]], channel_multiplier=1).then_inc(consts, 1)
            pool.iota(iota_i[:, :], pattern=[[1, P]], base=0, channel_multiplier=0).then_inc(consts, 1)
            for k in range(BUFS):
                pool.memset(got[k][:, MAIN:TILES, 0:2 * D], 0.0).then_inc(consts, 1)

            for k in range(PIECES):
                pool.wait_ge(x_in[k], 16 if k < PIECES - 1 else 32)
                a, z = k * PIECE, (k + 1) * PIECE if k < PIECES - 1 else BLOCKS
                pool.tensor_copy(hx[:, a:z, D:2 * D], x_piece[k][:, 0:z - a, :]).then_inc(x_set, 1)
            pool.wait_ge(x_set, PIECES)

            pool.wait_ge(row_ready, 1)
            pool.indirect_dma_start(rows_i[0:BLOCKS + 1, :], None, dst.rearrange("(r c) -> r c", r=ROWS),
                                    bass.IndirectOffsetOnAxis(ap=row_idx[0:BLOCKS + 1, :], axis=0),
                                    bounds_check=ROWS - 1, oob_is_err=True).then_inc(rows_got, 16)
            pool.memset(sel[:, :, :], 1.0).then_inc(consts, 1)
            pool.wait_ge(consts, 12)
            pool.affine_select(out=sel[:, :, :], in_=sel[:, :, :], compare_op=ALU.is_ge, fill=0.0,
                               base=0, pattern=[[-3, TILES], [0, P]], channel_multiplier=1).then_inc(consts, 1)
            pool.wait_ge(consts, 13)
            pool.affine_select(out=sel[:, :, :], in_=sel[:, :, :], compare_op=ALU.is_ge, fill=0.0,
                               base=2, pattern=[[3, TILES], [0, P]], channel_multiplier=-1).then_inc(consts, 1)
            pool.wait_ge(consts, 14)

            pool.wait_ge(windows_ready, 1)
            pool.wait_ge(table_out, 16 * (len(STEPS) + 1))
            pool.wait_ge(xT_ps, len(STEPS))

            def gather(third, before, prev, b, nxt, ahead):
                if follows(b, BUFS):
                    pool.wait_ge(summed[0], b.n - (BUFS - 1))
                pool.wait_ge(index_in[b.four], (b.fours + 1) * 64)
                n = pool.value_load(count_i[0:1, b.n:b.n + 1] if b.known else count_i[0:1, bass.ds(b.n, 1)],
                                    min_val=0, max_val=E)
                for c, tiles in enumerate(CHUNKS):
                    if c and follows(b, BUFS):
                        pool.wait_ge(consts, 14)
                        pool.wait_ge(summed[c], b.n - (BUFS - 1))
                    for g in tiles:
                        def rows():
                            pool.indirect_dma_start(got[b.four][:, g, 0:2 * D], None, table,
                                                    bass.IndirectOffsetOnAxis(ap=src_i[b.four][:, g:g + 1], axis=0),
                                                    bounds_check=N - 1, oob_is_err=True)\
                                .then_inc(gathered[b.four][c], 16)
                        if g <= MAIN:
                            rows()
                        else:
                            with pool.If(n > g * P):
                                rows()
                            with pool.Else():
                                pool.inc_swdge_sem([gathered[b.four][c]], [16], mode="add")

            pipeline(pool, gather)

        @block.scalar
        def _(act):
            act.wait_ge(w_ps, 1)
            act.activation(watt2T[:, :], ps_misc[:, 0:P], ACT.Copy).then_inc(w_sb, 1)

            def copy_xT(s):
                n = len(STEPS[s]) * D
                act.wait_ge(xT_ps, s + 1)
                if s >= 2:
                    act.wait_ge(h_ps, s - 1)
                act.activation(xT[s % 2][:, 0:n], ps_hd[s % 2][:, 0:n], ACT.Copy).then_inc(xT_sb, 1)

            for s in range(len(STEPS)):
                copy_xT(s)
                if s == 4:
                    act.wait_ge(first_ps, 1)
                    act.activation(first_row[0:1, :], ps_acc[0:1, 0:P], ACT.Copy).then_inc(first_sb, 1)
            act.wait_ge(w_ps, 2)
            act.activation(w12T[:, :], ps_misc[:, 0:D], ACT.Copy).then_inc(w_sb, 1)

            def copy_hot(b, chunks):
                for c in chunks:
                    a, z = cols(c)
                    act.wait_ge(other_ps[c], b.n + 1)
                    ps = ps_other[(b.two + c) % 2][:, 0:(z - a) * P].rearrange("p (g e) -> p g e", e=P)
                    act.activation(hotT[b.four][:, a:z, :], ps, ACT.Copy, bias=1.0, scale=-1.0)\
                        .then_inc(hot_sb[c], 1)

            def tanh(b, c):
                a, z = cols(c)
                act.wait_ge(added[c], b.n + 1)
                act.activation(edge[b.two][:, a:z, :], edge[b.two][:, a:z, :], ACT.Tanh).then_inc(tanh_done[c], 1)

            def weigh(b, chunks):
                for c in chunks:
                    if c == 0:
                        act.wait_ge(arg_done, b.n + 1)
                    if follows(b, 1):
                        act.wait_ge(summed[c], b.n)
                    for g in CHUNKS[c]:
                        last = act.activation(weight[:, g, :], other[b.four][:, g, :], ACT.Exp,
                                              bias=arg[b.two][:, g:g + 1], scale=-MASKED)
                    last.then_inc(weights_done[c], 1)

            def copy_scores(b):
                act.wait_ge(sT_ps, b.n + 1)
                act.activation(score3T[:, :], a_sT, ACT.Copy).then_inc(sT_sb, 1)

            def copy_sum_prod(b):
                act.wait_ge(spT_ps, b.n + 1)
                act.activation(sum_prodT[:, :], m_spT, ACT.Copy).then_inc(spT_sb, 1)

            def deviations(a, z):
                act.activation(std[:, a:z], stats[:, a:z, 1], ACT.Sqrt, bias=eps_col[:, 0:1]).then_inc(std_ready, 1)

            copy_hot(at_block(0, 0), range(NC))

            def step(third, before, prev, b, nxt, ahead):
                if exists(before):
                    weigh(before, (0,))
                if exists(prev):
                    copy_scores(prev)
                tanh(b, 0)
                if exists(before):
                    weigh(before, (1,))
                tanh(b, 1)
                if exists(before):
                    weigh(before, (2, 3))
                tanh(b, 2)
                if exists(before):
                    weigh(before, (4,))
                if exists(nxt):
                    copy_hot(nxt, (0, 1))
                tanh(b, 3)
                if exists(nxt):
                    copy_hot(nxt, (2,))
                if exists(before):
                    copy_sum_prod(before)
                tanh(b, 4)
                if exists(nxt):
                    copy_hot(nxt, (3, 4))

            pipeline(act, step)
            last, prev = at_block(0, LAST), at_block(0, LAST - 1)
            copy_scores(last)
            weigh(prev, range(NC))
            copy_sum_prod(prev)
            act.wait_ge(y_done, EARLY)
            deviations(0, EARLY)
            weigh(last, range(NC))
            copy_sum_prod(last)
            act.wait_ge(y_done, BLOCKS)
            deviations(EARLY, BLOCKS)

        @block.tensor
        def _(pe):
            pe.wait_ge(consts, 6)
            pe.wait_ge(watt_in, 32)
            pe.transpose(ps_misc[:, 0:P], watt2[:, :], ident[:, :]).then_inc(w_ps, 1)

            def transpose_x(s):
                if s % (PIECE // STEP) == 0 and s // (PIECE // STEP) < PIECES:
                    k = s // (PIECE // STEP)
                    pe.wait_ge(x_in[k], 16 if k < PIECES - 1 else 32)
                if s >= 2:
                    pe.wait_ge(xT_sb, s - 1)
                for k in range(0, len(STEPS[s]), 2):
                    b = STEPS[s][k]
                    p = min(b // PIECE, PIECES - 1)
                    last = pe.transpose(ps_hd[s % 2][:, k * D:(k + 2) * D], 
                                        x_piece[p][:, b - p * PIECE:b - p * PIECE + 2, :].rearrange("p b d -> p (b d)"),
                                        ident[:, :])
                last.then_inc(xT_ps, 1)

            def project(s):
                pe.wait_ge(xT_sb, s + 1)
                if s >= 2:
                    pe.wait_ge(h_sb, s - 1)
                for k in range(0, len(STEPS[s]), 2):
                    last = pe.matmul(ps_sc[s % 2][:, k * D:(k + 2) * D], xT[s % 2][:, k * D:(k + 2) * D],
                                     watt2T[:, :], start=True, stop=True)
                last.then_inc(h_ps, 1)

            for s in range(len(STEPS)):
                transpose_x(s)
                if s == 0:
                    pe.wait_ge(w_sb, 1)
                if s >= 1:
                    project(s - 1)
                if s == 1:
                    pe.wait_ge(rows_counted, 1)
                    pe.matmul(ps_acc[0:BLOCKS + 1, 0:1], below_row[0:ROWS, 0:BLOCKS + 1], ones[0:ROWS, :],
                              start=True, stop=True).then_inc(row_ps, 1)
                if s == 4:
                    pe.wait_ge(first_ready, 1)
                    pe.transpose(ps_acc[0:1, 0:P], first[:, :], ident[:, :]).then_inc(first_ps, 1)
            project(len(STEPS) - 1)
            pe.wait_ge(w12_in, 32)
            pe.transpose(ps_misc[:, 0:D], w12[:, :, :].rearrange("o a i -> o (a i)"),
                         ident[0:D, 0:D]).then_inc(w_ps, 1)

            def transpose_other(b, chunks):
                if 0 in chunks:
                    pe.wait_ge(other_built, b.n + 1)
                for c in chunks:
                    if c >= 2:
                        pe.wait_ge(hot_sb[c - 2], b.n + 1)
                    elif follows(b, 1):
                        pe.wait_ge(hot_sb[c - 2 + NC], b.n)
                    for k, g in enumerate(CHUNKS[c]):
                        last = pe.transpose(ps_other[(b.two + c) % 2][:, k * P:(k + 1) * P],
                                            other[b.four][:, g, :], ident16[:, :])
                    last.then_inc(other_ps[c], 1)

            def expand(b, c):
                pe.wait_ge(hot_sb[c], b.n + 1)
                if c >= 2:
                    pe.wait_ge(scored[c - 2], b.n + 1)
                elif follows(b, 1):
                    pe.wait_ge(scored[c - 2 + NC], b.n)
                for k, g in enumerate(CHUNKS[c]):
                    for part in range(3):
                        rhs = h3[:, b.n, part, :] if b.known else \
                            h3[:, bass.ds(b.n, 1), part, :].rearrange("p a d -> p (a d)")
                        last = pe.matmul(ps_hd[(b.two + c) % 2][:, k * D:(k + 1) * D], hotT[b.four][:, g, :], rhs,
                                         start=(part == 0), stop=(part == 2))
                last.then_inc(hd_ready[c], 1)

            def transpose_scores(b):
                pe.wait_ge(consts, 14)
                pe.wait_ge(split_done, b.n + 1)
                pe.transpose(a_sT, score3[:, :, :].rearrange("p g s -> p (g s)"), ident16[:, :]).then_inc(sT_ps, 1)

            def spread_scores(b, chunks):
                pe.wait_ge(sT_sb, b.n + 1)
                for c in chunks:
                    if c >= 2:
                        pe.wait_ge(sc_used[c - 2], b.n + 1)
                    elif follows(b, 1):
                        pe.wait_ge(sc_used[c - 2 + NC], b.n)
                    for k, g in enumerate(CHUNKS[c]):
                        spread = ps_sc[(b.two + c) % 2][:, k * P:(k + 1) * P]
                        pe.matmul(spread, other[b.four][:, g, :], mask16[:, :], start=True, stop=False)
                        last = pe.matmul(spread, sel[:, g, :], score3T[:, :], start=False, stop=True)
                    last.then_inc(sc_ready[c], 1)

            def spread_max(b):
                pe.wait_ge(max_split, b.n + 1)
                for g in range(TILES):
                    last = pe.matmul(m_max[:, 3 * g:3 * g + 3], hotT[b.four][:, g, :], max3[:, :],
                                     start=True, stop=True)
                last.then_inc(max_ps, 1)

            def sum_edges(b, chunks):
                for c in chunks:
                    if c == 0 and follows(b, 1):
                        pe.wait_ge(own["z1"], b.n)
                    pe.wait_ge(weights_done[c], b.n + 1)
                    for g in CHUNKS[c]:
                        last = pe.matmul(a_sum, weight[:, g, :], got[b.four][:, g, D:2 * D + 1],
                                         start=(g == 0), stop=(g == TILES - 1))
                    last.then_inc(summed[c], 1)

            def transpose_sum_prod(b):
                pe.wait_ge(sp_done, b.n + 1)
                pe.transpose(m_spT, sum_prod[:, :], ident[:, :]).then_inc(spT_ps, 1)

            def dense(b):
                pe.wait_ge(spT_sb, b.n + 1)
                pe.matmul(a_out, sum_prodT[:, :], w12T[:, :], start=True, stop=True).then_inc(out_ps, 1)

            transpose_other(at_block(0, 0), range(NC))
            pe.wait_ge(h3_ready, 1)
            pe.wait_ge(ones_set, BUFS)
            pe.wait_ge(w_sb, 2)

            def step(third, before, prev, b, nxt, ahead):
                if exists(third):
                    dense(third)
                expand(b, 0)
                if exists(prev):
                    transpose_scores(prev)
                expand(b, 1)
                if exists(prev):
                    spread_scores(prev, (0, 1))
                if exists(before):
                    sum_edges(before, (0,))
                if exists(prev):
                    spread_scores(prev, (2, 3))
                if exists(before):
                    sum_edges(before, (1,))
                if exists(prev):
                    spread_scores(prev, (4,))
                expand(b, 2)
                if exists(before):
                    sum_edges(before, (2, 3))
                if exists(nxt):
                    transpose_other(nxt, (0, 1))
                if exists(prev):
                    spread_max(prev)
                if exists(before):
                    sum_edges(before, (4,))
                expand(b, 3)
                if exists(nxt):
                    transpose_other(nxt, (2,))
                if exists(before):
                    transpose_sum_prod(before)
                expand(b, 4)
                if exists(nxt):
                    transpose_other(nxt, (3, 4))

            pipeline(pe, step)
            last, prev = at_block(0, LAST), at_block(0, LAST - 1)
            dense(at_block(0, LAST - 2))
            transpose_scores(last)
            spread_scores(last, range(NC))
            sum_edges(prev, range(NC))
            spread_max(last)
            transpose_sum_prod(prev)
            dense(prev)
            sum_edges(last, range(NC))
            transpose_sum_prod(last)
            dense(last)

        @block.vector
        def _(dve):
            done = [0]

            def link(ins):
                done[0] += 1
                ins.then_inc(dve_c, 1)
                dve.wait_ge(dve_c, done[0])

            dve.memset(ones[:, :], 1.0)
            dve.memset(eps_col[:, :], EPS_NORM)
            dve.memset(first[:, :], 0.0)
            dve.memset(base[:, :], 0.0)
            dve.wait_ge(consts, 4)
            dve.tensor_copy(bound[:, :], bound_i[:, :])
            link(dve.tensor_copy(bound_row[:, :], bound_row_i[:, :]))
            dve.wait_ge(rows_in, 16)
            link(dve.tensor_copy(row_last[0:ROWS, :], rows_i[0:ROWS, SEARCH_ROW - 1:SEARCH_ROW]))
            dve.tensor_scalar(below_row[0:ROWS, :], bound_row[0:ROWS, :], row_last[0:ROWS, 0:1], None,
                              ALU.is_gt).then_inc(rows_counted, 1)
            dve.wait_ge(consts, 7)
            dve.tensor_copy(ident16[:, :], ident[:, :])
            dve.tensor_scalar(mask16[:, :], ident[:, :], -MASKED, None, ALU.mult)
            link(dve.tensor_copy(iota_h[:, :], iota_i[:, :]))

            BOUNDS = BLOCKS + 1

            def pick_rows():
                dve.wait_ge(row_ps, 1)
                link(dve.tensor_scalar(row_f[0:BOUNDS, :], ps_acc[0:BOUNDS, 0:1], float(ROWS - 1), None, ALU.min))
                dve.tensor_copy(row_idx[0:BOUNDS, :], row_f[0:BOUNDS, :]).then_inc(row_ready, 1)

            def find_first():
                dve.wait_ge(rows_got, 16)
                link(dve.tensor_scalar(below[0:BOUNDS, :], rows_i[0:BOUNDS, :], bound[0:BOUNDS, 0:1], None,
                                       ALU.is_lt))
                link(dve.tensor_reduce(below_n[0:BOUNDS, :], below[0:BOUNDS, :], AX.X, ALU.add))
                dve.scalar_tensor_tensor(out=first[0:BOUNDS, :], in0=row_f[0:BOUNDS, :], scalar=float(SEARCH_ROW),
                                         in1=below_n[0:BOUNDS, :], op0=ALU.mult, op1=ALU.add)\
                    .then_inc(first_ready, 1)

            def set_windows():
                dve.wait_ge(first_sb, 1)
                link(dve.tensor_scalar(start_row[:, :], first_row[:, :], float(E - WINDOW), None, ALU.min))
                link(dve.tensor_tensor(count_row[:, 0:BLOCKS], first_row[:, 1:BOUNDS], start_row[:, 0:BLOCKS],
                                       ALU.subtract))
                link(dve.tensor_copy(start_i[:, 0:BLOCKS], start_row[:, 0:BLOCKS]))
                dve.tensor_copy(count_i[:, 0:BLOCKS], count_row[:, 0:BLOCKS]).then_inc(windows_ready, 1)

            def step_h(s):
                a, z = STEPS[s][0], STEPS[s][-1] + 1
                h = hx[:, a:z, 0:D]
                r = [t[:, 0:(z - a) * D].rearrange("p (b d) -> p b d", d=D) for t in hrest]
                dve.wait_ge(h_ps, s + 1)
                dve.tensor_tensor(h, ps_sc[s % 2][:, 0:(z - a) * D].rearrange("p (b d) -> p b d", d=D),
                                  batt_bc[:, :].rearrange("p (a d) -> p a d", a=1).to_broadcast([P, z - a, D]),
                                  ALU.add).then_inc(h_sb, 1)
                dve.wait_ge(h_sb, s + 1)
                link(dve.tensor_scalar(h3[:, a:z, 0, :], h, SCALE, None, ALU.mult))
                link(dve.scalar_tensor_tensor(out=r[0], in0=h, scalar=SCALE, in1=h3[:, a:z, 0, :],
                                              op0=ALU.mult, op1=ALU.subtract))
                link(dve.tensor_copy(h3[:, a:z, 1, :], r[0]))
                link(dve.tensor_tensor(r[1], r[0], h3[:, a:z, 1, :], ALU.subtract))
                link(dve.tensor_copy(h3[:, a:z, 2, :], r[1]))

            dve.wait_ge(bias_in, 48)
            for s in range(len(STEPS)):
                step_h(s)
                if s == 0:
                    pick_rows()
                if s == 2:
                    find_first()
                if s == 4:
                    set_windows()
            dve.tensor_tensor(b12[:, :], b1_bc[:, :], b2_bc[:, :], ALU.add).then_inc(h3_ready, 1)
            dve.wait_ge(h3_ready, 1)
            dve.wait_ge(x_set, PIECES)
            dve.wait_ge(xT_ps, len(STEPS))
            for k in range(BUFS):
                dve.memset(got[k][:, :, 2 * D:2 * D + 1], 1.0).then_inc(ones_set, 1)

            def chain(name, ins, b):
                ins.then_inc(own[name], 1)
                dve.wait_ge(own[name], b.n + 1)

            def build_other(b):
                dve.wait_ge(index_in[b.four], (b.fours + 1) * 64)
                if follows(b, BUFS):
                    dve.wait_ge(weights_done[NC - 1], b.n - (BUFS - 1))
                chain("rel", dve.tensor_scalar(
                    dst_rel[:, :, :], dst_i[b.four][:, :].rearrange("p (g a) -> p g a", a=1).to_broadcast([P, TILES, 2]),
                    base[:, 0:1], None, ALU.subtract), b)
                chain("base", dve.tensor_scalar(base[:, :], base[:, :], float(P), None, ALU.add), b)
                dve.tensor_tensor(
                    other[b.four][:, :, :].rearrange("p g (n a) -> p g n a", a=2),
                    iota_h[:, :].rearrange("p (z n a) -> p z n a", z=1, a=2).to_broadcast([P, TILES, P // 2, 2]),
                    dst_rel[:, :, :].rearrange("p g (z a) -> p g z a", z=1).to_broadcast([P, TILES, P // 2, 2]),
                    ALU.not_equal).then_inc(other_built, 1)

            def add(b, c):
                a, z = cols(c)
                if c == 0:
                    dve.wait_ge(edge_in[b.two], (b.twos + 1) * 32)
                dve.wait_ge(gathered[b.four][c], (b.fours + 1) * (16 * (z - a)))
                dve.tensor_tensor(edge[b.two][:, a:z, :], edge[b.two][:, a:z, :], got[b.four][:, a:z, 0:D],
                                  ALU.add).then_inc(added[c], 1)

            def dot(b, c):
                a, z = cols(c)
                dve.wait_ge(consts, 14)
                dve.wait_ge(tanh_done[c], b.n + 1)
                dve.wait_ge(hd_ready[c], b.n + 1)
                for k, g in enumerate(CHUNKS[c]):
                    last = dve.tensor_tensor_reduce(
                        out=edge[b.two][:, g, :], in0=edge[b.two][:, g, :],
                        in1=ps_hd[(b.two + c) % 2][:, k * D:(k + 1) * D], scale=1.0, scalar=0.0,
                        op0=ALU.mult, op1=ALU.add, accum_out=raw[b.two][:, g:g + 1])
                last.then_inc(scored[c], 1)

            def finish_scores(b):
                dve.wait_ge(scored[NC - 1], b.n + 1)
                chain("score", dve.scalar_tensor_tensor(out=score[:, :], in0=raw[b.two][:, :], scalar=SLOPE,
                                                        in1=raw[b.two][:, :], op0=ALU.mult, op1=ALU.max), b)
                chain("s0", dve.tensor_copy(score3[:, :, 0], score[:, :]), b)
                chain("r1", dve.tensor_tensor(rest1[:, :], score[:, :], score3[:, :, 0], ALU.subtract), b)
                chain("s1", dve.tensor_copy(score3[:, :, 1], rest1[:, :]), b)
                chain("r2", dve.tensor_tensor(rest2[:, :], rest1[:, :], score3[:, :, 1], ALU.subtract), b)
                dve.tensor_copy(score3[:, :, 2], rest2[:, :]).then_inc(split_done, 1)

            def take_max(b, chunks):
                for c in chunks:
                    a, z = cols(c)
                    dve.wait_ge(sc_ready[c], b.n + 1)
                    dve.tensor_reduce(chunk_max[:, c:c + 1], ps_sc[(b.two + c) % 2][:, 0:(z - a) * P], AX.X, ALU.max)\
                        .then_inc(sc_used[c], 1)

            def split_max(b):
                dve.wait_ge(sc_used[NC - 1], b.n + 1)
                chain("nmax", dve.tensor_reduce(node_max[:, :], chunk_max[:, :], AX.X, ALU.max), b)
                chain("m0", dve.tensor_copy(max3[:, 0:1], node_max[:, :]), b)
                chain("q1", dve.tensor_tensor(mrest1[:, :], node_max[:, :], max3[:, 0:1], ALU.subtract), b)
                chain("m1", dve.tensor_copy(max3[:, 1:2], mrest1[:, :]), b)
                chain("q2", dve.tensor_tensor(mrest2[:, :], mrest1[:, :], max3[:, 1:2], ALU.subtract), b)
                dve.tensor_copy(max3[:, 2:3], mrest2[:, :]).then_inc(max_split, 1)

            def exponents(b):
                dve.wait_ge(max_ps, b.n + 1)
                if follows(b, 2):
                    dve.wait_ge(weights_done[NC - 1], b.n - 1)
                chain("emax", dve.tensor_reduce(edge_max[:, :], m_max.rearrange("p (g s) -> p g s", s=3),
                                                AX.X, ALU.add), b)
                dve.tensor_tensor(arg[b.two][:, :], score[:, :], edge_max[:, :], ALU.subtract).then_inc(arg_done, 1)

            def neighbours(b):
                dve.wait_ge(summed[NC - 1], b.n + 1)
                chain("den", dve.tensor_scalar(den[:, :], a_sum[:, D:D + 1], EPS_ALPHA, None, ALU.add), b)
                chain("rden", dve.reciprocal(rden[:, :], den[:, :]), b)
                dve.tensor_scalar(h_neigh[:, :], a_sum[:, 0:D], rden[:, 0:1], None, ALU.mult)\
                    .then_inc(h_neigh_done, 1)
                dve.wait_ge(h_neigh_done, b.n + 1)
                xb = node_rows(hx, b, D, 2 * D)
                dve.tensor_tensor(sum_prod[:, 0:D], h_neigh[:, :], xb, ALU.add)
                dve.tensor_tensor(sum_prod[:, D:2 * D], h_neigh[:, :], xb, ALU.mult).then_inc(sp_done, 1)

            def residual(b, part):
                if part == 0:
                    dve.wait_ge(out_ps, b.n + 1)
                    dve.tensor_tensor(z1[:, :], a_out, b12[:, :], ALU.add).then_inc(own["z1"], 1)
                    return
                dve.wait_ge(own["z1"], b.n + 1)
                chain("z2", dve.scalar_tensor_tensor(out=z2[:, :], in0=z1[:, :], scalar=SLOPE, in1=z1[:, :],
                                                     op0=ALU.mult, op1=ALU.max), b)
                chain("y", dve.tensor_tensor(y_new[:, :], node_rows(hx, b, D, 2 * D), z2[:, :], ALU.add), b)
                dve.bn_stats(bn6[:, :], y_new[:, :]).then_inc(own["bn"], 1)
                dve.tensor_copy(node_rows(hx, b, 0, D), y_new[:, :])
                dve.wait_ge(consts, 14)
                dve.wait_ge(own["bn"], b.n + 1)
                chain("aggr", dve.bn_aggr(mean_var[:, :], bn6[:, :]), b)
                dve.tensor_copy(node_rows(stats, b, 0, 2), mean_var[:, :]).then_inc(y_done, 1)

            def normalise(k):
                a, z = NORMED[k]
                if k in (0, len(NORMED) - 1):
                    s = 0 if k == 0 else 1
                    dve.wait_ge(std_ready, s + 1)
                    dve.reciprocal(rstd[:, a:(EARLY, BLOCKS)[s]], std[:, a:(EARLY, BLOCKS)[s]]).then_inc(rstd_ready, 1)
                    dve.wait_ge(rstd_ready, s + 1)
                y = hx[:, a:z, 0:D]
                dve.tensor_tensor(y, y, stats[:, a:z, 0:1].to_broadcast([P, z - a, D]), ALU.subtract)\
                    .then_inc(centred, 1)
                dve.wait_ge(centred, k + 1)
                dve.tensor_tensor(y, y, rstd[:, a:z].rearrange("p (b a) -> p b a", a=1).to_broadcast([P, z - a, D]),
                                  ALU.mult).then_inc(normed, 1)

            build_other(at_block(0, 0))

            def step(third, before, prev, b, nxt, ahead):
                if exists(third):
                    residual(third, 0)
                if exists(prev):
                    finish_scores(prev)
                if exists(third):
                    residual(third, 1)
                add(b, 0)
                if exists(prev):
                    take_max(prev, (0,))
                add(b, 1)
                if exists(prev):
                    take_max(prev, (1,))
                dot(b, 0)
                if exists(prev):
                    take_max(prev, (2,))
                add(b, 2)
                if exists(prev):
                    take_max(prev, (3,))
                dot(b, 1)
                if exists(prev):
                    take_max(prev, (4,))
                    split_max(prev)
                if exists(nxt):
                    build_other(nxt)
                dot(b, 2)
                add(b, 3)
                if exists(prev):
                    exponents(prev)
                if exists(before):
                    neighbours(before)
                dot(b, 3)
                add(b, 4)
                dot(b, 4)

            pipeline(dve, step)
            last, prev = at_block(0, LAST), at_block(0, LAST - 1)
            residual(at_block(0, LAST - 2), 0)
            finish_scores(last)
            residual(at_block(0, LAST - 2), 1)
            take_max(last, range(NC))
            split_max(last)
            exponents(last)
            neighbours(prev)
            residual(prev, 0)
            residual(prev, 1)
            for k in range(3):
                normalise(k)
            neighbours(last)
            residual(last, 0)
            residual(last, 1)
            normalise(3)


_INS = ['x', 'src', 'dst', 'edge_attr_64', 'L0_gnn_W1_w', 'L0_gnn_W1_b', 'L0_gnn_W2_w', 'L0_gnn_W2_b',
        'L0_gnn_Watt_w', 'L0_gnn_Watt_b']


def kernel(**inputs):
    import numpy as _np
    import concourse.bacc as _bacc
    from concourse.bass_utils import run_bass_kernel_spmd as _run

    nc = _bacc.Bacc("TRN2", target_bir_lowering=False, num_devices=1)
    arrays, args = {}, []
    for name in _INS:
        a = _np.ascontiguousarray(inputs[name])
        arrays[f"in_{name}"] = a
        args.append(nc.dram_tensor(f"in_{name}", a.shape, mybir.dt.from_np(a.dtype), kind="ExternalInput").ap())
    args.append(nc.dram_tensor("out_0", arrays["in_x"].shape, F32, kind="ExternalOutput").ap())
    gnn_layer(nc, *args)
    r = _run(nc, [arrays], core_ids=[0])
    return r.results[0]["out_0"]
```

```python
from collections import namedtuple
from contextlib import ExitStack

import concourse.bass as bass
from concourse import mybir

ALU = mybir.AluOpType
ACT = mybir.ActivationFunctionType
AX = mybir.AxisListType
F32 = mybir.dt.float32
BF16 = mybir.dt.bfloat16
I32 = mybir.dt.int32

P = 128
MAIN = 16
TAIL = 3
TILES = MAIN + TAIL
CHUNK = 4
BUFS = 4
SEARCH_ROW = 1700
STEP = 8
PIECES = 4
MASKED = float(2 ** 100)
LOWEST = -3.0e38
SLOPE = 0.2
EPS_ALPHA = 1e-9
EPS_NORM = 1e-5

Block = namedtuple("Block", "n four two fours twos known")


def at_block(turn, k):
    return Block(turn * BUFS + k, k % BUFS, k % 2, turn + k // BUFS, turn * 2 + k // 2, isinstance(turn, int))


def gnn_layer(nc, x, src, dst, edge_attr, w1, b1, w2, b2, watt, batt, out):
    N, D = x.shape
    E, = src.shape
    BLOCKS = (N + P - 1) // P
    LAST = BLOCKS - 1
    LAST_NODES = N - LAST * P
    WINDOW = TILES * P
    ROWS = E // SEARCH_ROW
    CHUNKS = [range(a, min(a + CHUNK, TILES)) for a in range(0, TILES, CHUNK)]
    NC = len(CHUNKS)
    STEPS = [range(a, min(a + STEP, BLOCKS)) for a in range(0, BLOCKS, STEP)]
    ROW_STEP, FIRST_STEP, WINDOW_STEP = 0, 11, 12
    LAG = 13
    PIECE = STEP * (len(STEPS) // PIECES)
    TURNS = (BLOCKS - 2) // BUFS
    EARLY = LAST - 4
    DEVIATED = [(0, EARLY), (EARLY, LAST), (LAST, BLOCKS)]
    POOLED = [(0, EARLY // 2), (EARLY // 2, EARLY)]
    NORMED = [(EARLY, LAST), (LAST, BLOCKS)]
    SCALE = D ** -0.5
    LANES = ROWS
    STATE = D + 2
    assert BLOCKS * P + P >= N + LANES and (BLOCKS - (PIECES - 1) * PIECE) * STATE <= TILES * (2 * D + 1)
    assert D == 64 and ROWS * SEARCH_ROW == E and TURNS * BUFS + 2 == BLOCKS and BLOCKS % 2 == 0
    assert (BLOCKS - (PIECES - 1) * PIECE) * D <= MAIN * (2 * D + 1) and BUFS == PIECES
    assert BLOCKS + 1 <= P and ROWS <= P and WINDOW <= E and LAST_NODES > 0

    with ExitStack() as ctx:
        def sb(name, shape, dt=F32):
            return ctx.enter_context(nc.sbuf_tensor(name, shape, dt))

        def bank(name, dt=F32):
            return ctx.enter_context(nc.psum_tensor(name, [P, 512 * 4 // mybir.dt.size(dt)], dt))

        def sem(name):
            return ctx.enter_context(nc.semaphore(name))

        def by_chunk(name):
            return [sem(f"{name}_{c}") for c in range(NC)]

        table = nc.dram_tensor("table", (N, 2 * D), F32, kind="Internal").ap()

        state = nc.dram_tensor("state", (BLOCKS * P + P, STATE), F32, kind="Internal").ap()

        hx = sb("hx", [P, BLOCKS, 2 * D])
        h3 = sb("h3", [P, BLOCKS, 3, D], BF16)
        stats = sb("stats", [P, BLOCKS, 2])
        std = sb("std", [P, BLOCKS])
        rstd = sb("rstd", [P, BLOCKS])
        ident = sb("ident", [P, P])
        ident16 = sb("ident16", [P, P], BF16)
        mask16 = sb("mask16", [P, P], BF16)
        iota_h = sb("iota_h", [P, P], BF16)
        iota_i = sb("iota_i", [P, P], I32)
        sel = sb("sel", [3 * TILES, TILES, P], BF16)
        watt2 = sb("watt2", [P, P])
        watt2T = sb("watt2T", [P, P])
        w12 = sb("w12", [D, 2, D])
        w12T = sb("w12T", [P, D])
        batt_bc = sb("batt_bc", [P, D])
        b1_bc = sb("b1_bc", [P, D])
        b2_bc = sb("b2_bc", [P, D])
        b12 = sb("b12", [P, D])
        eps_col = sb("eps_col", [P, 1])
        ones = sb("ones", [P, 1])

        bound_i = sb("bound_i", [P, 1], I32)
        bound = sb("bound", [P, 1])
        bound_row_i = sb("bound_row_i", [P, P], I32)
        bound_row = sb("bound_row", [P, P])
        row_last = sb("row_last", [P, 1])
        below_row = sb("below_row", [P, P])
        row_f = sb("row_f", [P, 1])
        row_idx = sb("row_idx", [P, 1], I32)
        below_n = sb("below_n", [P, 1])
        first = sb("first", [P, 1])
        first_row = sb("first_row", [1, P + 1])
        next_first = sb("next_first", [P, 1], I32)
        falls = sb("falls", [P, 1])
        row_falls = sb("row_falls", [P, 1])
        over_row = sb("over_row", [1, P])
        over = sb("over", [1, 1])
        general = sb("general", [1, 1])
        general_i = sb("general_i", [1, 1], I32)
        start_row = sb("start_row", [1, P])
        count_row = sb("count_row", [1, P])
        start_i = sb("start_i", [1, P], I32)
        count_i = sb("count_i", [1, P], I32)

        src_i = [sb(f"src_i{k}", [P, TILES], I32) for k in range(BUFS)]
        dst_i = [sb(f"dst_i{k}", [P, TILES], I32) for k in range(BUFS)]
        edge = [sb(f"edge{k}", [P, TILES, D]) for k in range(2)]
        got = [sb(f"got{k}", [P, TILES, 2 * D + 1]) for k in range(BUFS)]
        other = [sb(f"other{k}", [P, TILES, P], BF16) for k in range(BUFS)]
        hotT = [sb(f"hotT{k}", [P, TILES, P], BF16) for k in range(BUFS)]
        raw = [sb(f"raw{k}", [P, TILES]) for k in range(2)]
        arg = [sb(f"arg{k}", [P, TILES]) for k in range(2)]
        base = sb("base", [P, 1])
        dst_rel = sb("dst_rel", [P, TILES, 2], BF16)
        product = sb("product", [P, D])
        score = sb("score", [P, TILES])
        score3 = sb("score3", [P, TILES, 3], BF16)
        rest1 = sb("rest1", [P, TILES])
        rest2 = sb("rest2", [P, TILES])
        score3T = sb("score3T", [3 * TILES, P], BF16)
        chunk_max = sb("chunk_max", [P, NC])
        node_max = sb("node_max", [P, 1])
        max3 = sb("max3", [P, 3], BF16)
        mrest1 = sb("mrest1", [P, 1])
        mrest2 = sb("mrest2", [P, 1])
        edge_max = sb("edge_max", [P, TILES])
        weight = sb("weight", [P, TILES, P])
        den = sb("den", [P, 1])
        rden = sb("rden", [P, 1])
        h_neigh = sb("h_neigh", [P, D])
        sum_prod = sb("sum_prod", [P, 2 * D])
        sum_prodT = sb("sum_prodT", [P, P])
        z1 = sb("z1", [P, D])
        z2 = sb("z2", [P, D])
        y_new = sb("y_new", [P, D])
        bn6 = sb("bn6", [P, 6])
        mean_var = sb("mean_var", [P, 2])
        rows_i = weight[:, :, :].rearrange("p g n -> p (g n)")[:, 0:SEARCH_ROW].bitcast(I32)
        below = hotT[1][:, :, :].rearrange("p g n -> p (g n)")[:, 0:SEARCH_ROW]
        xT = [edge[k][:, 0:STEP, :].rearrange("p g d -> p (g d)") for k in range(2)]
        x_piece = [t[:, :, :].rearrange("p g c -> p (g c)")[:, 0:(BLOCKS - (PIECES - 1) * PIECE) * D]
                   .rearrange("p (b d) -> p b d", d=D) for t in got]
        hrest = [[other[2 + j][:, 8 * k:8 * (k + 1), :].rearrange("p g n -> p (g n)").bitcast(F32) for k in range(2)]
                 for j in range(2)]

        falling = hotT[0][:, :, :].rearrange("p g n -> p (g n)")[:, 0:SEARCH_ROW - 1]
        taken = [0]

        def part(width, dt=F32):
            taken[0] += width
            view = weight[:, :, :].rearrange("p g n -> p (g n)")[0:LANES, taken[0] - width:taken[0]]
            return view if dt is F32 else view.bitcast(dt)

        g_src, g_dst, g_to = part(1, I32), part(1, I32), part(1, I32)
        g_edge, g_source, g_target = part(D), part(2 * D), part(2 * D)
        g_old, g_new, g_sent = part(STATE), part(STATE), part(D + 1)
        g_dst_f, g_slot, g_raw, g_scaled, g_score, g_most, g_rise, g_fade, g_earlier, g_move =\
            (part(1) for _ in range(10))
        g_arg, g_prob, g_keep = part(1), part(1), part(1)
        g_dst_wide, g_score_wide, g_same, g_far, g_before, g_lower = (part(LANES) for _ in range(6))
        state_piece = [t[:, :, :].rearrange("p g c -> p (g c)")[:, 0:(BLOCKS - (PIECES - 1) * PIECE) * STATE]
                       .rearrange("p (b d) -> p b d", d=STATE) for t in got]

        ps_hd = [bank(f"ps_hd{k}") for k in range(2)]
        ps_other = [bank(f"ps_other{k}", BF16) for k in range(2)]
        ps_sc = [bank(f"ps_sc{k}") for k in range(2)]
        ps_acc = bank("ps_acc")
        ps_misc = bank("ps_misc")
        a_sum = ps_acc[:, 0:D + 1]
        a_out = ps_acc[:, 128:128 + D]
        a_sT = ps_acc[0:3 * TILES, 256:256 + P // 2].bitcast(BF16)
        m_max = ps_misc[:, 0:3 * TILES]
        m_spT = ps_misc[:, 128:256]

        consts = sem("consts")
        x_in = [sem(f"x_in{k}") for k in range(PIECES)]
        next_in = sem("next_in")
        falls_ready = sem("falls_ready")
        x_set = sem("x_set")
        ones_set = sem("ones_set")
        watt_in = sem("watt_in")
        w12_in = sem("w12_in")
        batt_in = sem("batt_in")
        bias_in = sem("bias_in")
        rows_in = sem("rows_in")
        dve_c = sem("dve_c")
        w_ps = sem("w_ps")
        w_sb = sem("w_sb")
        rows_counted = sem("rows_counted")
        row_ps = sem("row_ps")
        row_ready = sem("row_ready")
        rows_got = sem("rows_got")
        first_ready = sem("first_ready")
        first_ps = sem("first_ps")
        first_sb = sem("first_sb")
        windows_ready = sem("windows_ready")
        xT_ps = sem("xT_ps")
        xT_sb = sem("xT_sb")
        h_ps = sem("h_ps")
        h_sb = sem("h_sb")
        part_done = [sem(f"part_done{k}") for k in range(3)]
        rest_done = [sem(f"rest_done{k}") for k in range(2)]
        table_out = sem("table_out")
        h3_ready = sem("h3_ready")
        index_in = [sem(f"index_in{k}") for k in range(BUFS)]
        edge_in = [sem(f"edge_in{k}") for k in range(2)]
        gathered = [[sem(f"gathered{k}_{c}") for c in range(NC)] for k in range(BUFS)]
        other_built = sem("other_built")
        other_ps = by_chunk("other_ps")
        hot_sb = by_chunk("hot_sb")
        hd_ready = by_chunk("hd_ready")
        added = by_chunk("added")
        tanh_done = by_chunk("tanh_done")
        scored = by_chunk("scored")
        split_done = sem("split_done")
        sT_ps = sem("sT_ps")
        sT_sb = sem("sT_sb")
        sc_ready = by_chunk("sc_ready")
        sc_used = by_chunk("sc_used")
        max_split = sem("max_split")
        max_ps = sem("max_ps")
        arg_done = sem("arg_done")
        weights_done = by_chunk("weights_done")
        summed = by_chunk("summed")
        h_neigh_done = sem("h_neigh_done")
        sp_done = sem("sp_done")
        spT_ps = sem("spT_ps")
        spT_sb = sem("spT_sb")
        out_ps = sem("out_ps")
        y_done = sem("y_done")
        own = {name: sem(f"dve_{name}") for name in
               ("rel", "base", "score", "s0", "r1", "s1", "r2", "nmax", "m0", "q1", "m1", "q2",
                "emax", "den", "rden", "z1", "z2", "y", "bn", "aggr")}
        g_lower_set, g_fresh = scored[0], scored[1]
        g_in = index_in[0], index_in[2], index_in[3]
        g_got = gathered[0][0:3]
        g_put = gathered[1][0]
        g_back = index_in[1]
        g_added, g_tanh_done = added[0], tanh_done[0]
        g_wide, g_wide_ps = split_done, sT_ps
        g_args, g_exps = arg_done, weights_done[0]
        g_sent_done, g_sums_ps, g_new_done = max_split, max_ps, sc_used[0]
        g_own = own["rel"]
        std_ready = sem("std_ready")
        rstd_ready = sem("rstd_ready")
        centred = sem("centred")
        normed = sem("normed")
        pool_centred = sem("pool_centred")
        pool_normed = sem("pool_normed")
        stored = sem("stored")

        block = ctx.enter_context(nc.Block())

        def pipeline(e, step):
            def turn(t, k):
                step(*(at_block(t, k + j) for j in (-3, -2, -1, 0, 1, 2)))

            for k in range(BUFS):
                turn(0, k)
            with e.Fori(1, TURNS) as t:
                for k in range(BUFS):
                    turn(t, k)
            for k in range(TURNS * BUFS, BLOCKS):
                turn(0, k)

        def exists(b):
            return not b.known or 0 <= b.n < BLOCKS

        def follows(b, n):
            return not b.known or b.n >= n

        def cols(c):
            return CHUNKS[c][0], CHUNKS[c][-1] + 1

        def node_rows(t, b, a, z):
            if b.known:
                return t[:, b.n, a:z]
            return t[:, bass.ds(b.n, 1), a:z].rearrange("p a d -> p (a d)")

        def h_rest(s, part):
            n = len(STEPS[s])
            return hrest[part][s % 2][:, 0:n * D].rearrange("p (b d) -> p b d", d=D)

        def normalise(e, a, z, centred, normed, count):
            y = hx[:, a:z, 0:D]
            e.tensor_tensor(y, y, stats[:, a:z, 0:1].to_broadcast([P, z - a, D]), ALU.subtract).then_inc(centred, 1)
            e.wait_ge(centred, count)
            e.tensor_tensor(y, y, rstd[:, a:z].rearrange("p (b a) -> p b a", a=1).to_broadcast([P, z - a, D]),
                            ALU.mult).then_inc(normed, 1)

        def is_general(e):
            e.wait_ge(windows_ready, 1)
            return e.value_load(general_i[0:1, 0:1], min_val=0, max_val=2 * E) > 0

        def piece_blocks(e, body):
            for k in range(PIECES):
                a, z = k * PIECE, (k + 1) * PIECE if k < PIECES - 1 else BLOCKS
                with e.Fori(0, z - a) as i:
                    body(Block(i + a, 0, 0, 0, 0, False), k, i)

        @block.sync
        def _(sp):
            def load_x(k):
                a, z = k * PIECE, (k + 1) * PIECE if k < PIECES - 1 else LAST
                sp.dma_start(x_piece[k][:, 0:z - a, :], x[a * P:z * P, :].rearrange("(b p) d -> p b d", p=P))\
                    .then_inc(x_in[k], 16)

            load_x(0)
            sp.wait_ge(consts, 2)
            for k in range(2):
                sp.dma_start(watt2[k * D:(k + 1) * D, k * D:(k + 1) * D], watt).then_inc(watt_in, 16)
            sp.dma_start(batt_bc[:, :], batt.rearrange("(a d) -> a d", a=1).to_broadcast([P, D]))\
                .then_inc(batt_in, 16)
            sp.dma_start(rows_i[0:ROWS, :], dst.rearrange("(r c) -> r c", r=ROWS)).then_inc(rows_in, 16)
            sp.dma_start(next_first[0:ROWS - 1, :], dst.rearrange("(r c) -> r c", r=ROWS)[1:ROWS, 0:1],
                         allow_slow_non_contiguous=True).then_inc(next_in, 16)
            for k in range(1, PIECES):
                load_x(k)
            sp.dma_start(x_piece[PIECES - 1][0:LAST_NODES, LAST - (PIECES - 1) * PIECE, :], x[LAST * P:N, :]).then_inc(x_in[PIECES - 1], 16)
            sp.dma_start(w12[:, 0, :], w1).then_inc(w12_in, 16)
            sp.dma_start(w12[:, 1, :], w2).then_inc(w12_in, 16)
            for tile, vector in ((b1_bc, b1), (b2_bc, b2)):
                sp.dma_start(tile[:, :], vector.rearrange("(a d) -> a d", a=1).to_broadcast([P, D]))\
                    .then_inc(bias_in, 16)
            for s, blocks in enumerate(STEPS):
                sp.wait_ge(x_set, min(s // (PIECE // STEP), PIECES - 1) + 1)
                sp.wait_ge(h_sb, s + 1)
                a, z = blocks[0], min(blocks[-1] + 1, LAST)
                sp.dma_start(table[a * P:z * P, :].rearrange("(b p) d -> p b d", p=P), hx[:, a:z, :])\
                    .then_inc(table_out, 16)
            sp.dma_start(table[LAST * P:N, :], hx[0:LAST_NODES, LAST, :]).then_inc(table_out, 16)


            def first_edge(b):
                return sp.value_load(start_i[0:1, b.n:b.n + 1] if b.known else start_i[0:1, bass.ds(b.n, 1)],
                                     min_val=0, max_val=E - WINDOW)

            def load_indices(b, o):
                for tile, vector in ((src_i[b.four], src), (dst_i[b.four], dst)):
                    sp.dma_start(tile[:, 0:MAIN], vector[bass.ds(o, MAIN * P)].rearrange("(p g) -> p g", g=MAIN))\
                        .then_inc(index_in[b.four], 16)
                    sp.dma_start(tile[:, MAIN:TILES],
                                 vector[bass.ds(o + MAIN * P, TAIL * P)].rearrange("(g p) -> p g", p=P),
                                 allow_slow_non_contiguous=True).then_inc(index_in[b.four], 16)

            def load_edges(b, o):
                sp.dma_start(edge[b.two][:, 0:MAIN, :],
                             edge_attr[bass.ds(o, MAIN * P), :].rearrange("(p g) d -> p g d", g=MAIN))\
                    .then_inc(edge_in[b.two], 16)
                sp.dma_start(edge[b.two][:, MAIN:TILES, :],
                             edge_attr[bass.ds(o + MAIN * P, TAIL * P), :].rearrange("(g p) d -> p g d", p=P))\
                    .then_inc(edge_in[b.two], 16)


            def step(third, before, prev, b, nxt, ahead):
                edges_at = first_edge(b)
                indices_at = first_edge(ahead) if exists(ahead) else None
                if follows(b, 2):
                    sp.wait_ge(scored[NC - 1], b.n - 1)
                load_edges(b, edges_at)
                if exists(ahead):
                    load_indices(ahead, indices_at)

            def general_tile(t):
                sp.wait_ge(g_put, (t + 1) * 16)
                sp.dma_start(g_edge, edge_attr.rearrange("(p c) d -> p c d", p=LANES)[:, bass.ds(t, 1), :]
                             .rearrange("p c d -> p (c d)")).then_inc(g_in[0], 16)
                for k, tile, vector in ((1, g_src, src), (2, g_dst, dst)):
                    sp.dma_start(tile, vector.rearrange("(p c) -> p c", p=LANES)[:, bass.ds(t, 1)],
                                 allow_slow_non_contiguous=True).then_inc(g_in[k], 16)

            with sp.If(is_general(sp)):
                with sp.Fori(0, E // LANES) as t:
                    general_tile(t)
                sp.wait_ge(g_put, (E // LANES + 1) * 16)
                for k in range(PIECES):
                    a, z = k * PIECE, (k + 1) * PIECE if k < PIECES - 1 else BLOCKS
                    sp.dma_start(state_piece[k][:, 0:z - a, :],
                                 state[a * P:z * P, :].rearrange("(b p) d -> p b d", p=P)).then_inc(g_back, 16)
            with sp.Else():
                for n in range(2):
                    load_indices(at_block(0, n), first_edge(at_block(0, n)))
                pipeline(sp, step)

            def store(a, z):
                sp.dma_start(out[a * P:z * P, :].rearrange("(b p) d -> p b d", p=P), hx[:, a:z, 0:D])\
                    .then_inc(stored, 16)

            for k, (a, z) in enumerate(POOLED):
                sp.wait_ge(pool_normed, k + 1)
                store(a, z)
            sp.wait_ge(normed, 1)
            store(EARLY, LAST)
            sp.wait_ge(normed, len(NORMED))
            sp.dma_start(out[LAST * P:N, :], hx[0:LAST_NODES, LAST, 0:D]).then_inc(stored, 16)
            sp.wait_ge(stored, 16 * (len(POOLED) + 2))

        @block.gpsimd
        def _(pool):
            pool.memset(watt2[:, :], 0.0).then_inc(consts, 1)
            pool.memset(x_piece[PIECES - 1][:, LAST - (PIECES - 1) * PIECE, :], 0.0).then_inc(consts, 1)
            pool.iota(bound_row_i[:, :], pattern=[[P, P]], base=0, channel_multiplier=0).then_inc(consts, 1)
            pool.iota(bound_i[:, :], pattern=[[0, 1]], base=0, channel_multiplier=P).then_inc(consts, 1)
            pool.memset(ident[:, :], 0.0).then_inc(consts, 1)
            pool.wait_ge(consts, 5)
            pool.affine_select(out=ident[:, :], in_=ident[:, :], compare_op=ALU.not_equal, fill=1.0,
                               base=0, pattern=[[-1, P]], channel_multiplier=1).then_inc(consts, 1)
            pool.iota(iota_i[:, :], pattern=[[1, P]], base=0, channel_multiplier=0).then_inc(consts, 1)
            for k in range(BUFS):
                pool.memset(got[k][:, MAIN:TILES, 0:2 * D], 0.0).then_inc(consts, 1)

            def place_x(k):
                pool.wait_ge(x_in[k], 16 if k < PIECES - 1 else 32)
                a, z = k * PIECE, (k + 1) * PIECE if k < PIECES - 1 else BLOCKS
                pool.tensor_copy(hx[:, a:z, D:2 * D], x_piece[k][:, 0:z - a, :]).then_inc(x_set, 1)

            place_x(0)
            pool.wait_ge(row_ready, 1)
            pool.indirect_dma_start(rows_i[0:BLOCKS + 1, :], None, dst.rearrange("(r c) -> r c", r=ROWS),
                                    bass.IndirectOffsetOnAxis(ap=row_idx[0:BLOCKS + 1, :], axis=0),
                                    bounds_check=ROWS - 1, oob_is_err=True).then_inc(rows_got, 16)
            for k in range(1, PIECES):
                place_x(k)
            pool.wait_ge(x_set, PIECES)

            pool.memset(sel[:, :, :], 1.0).then_inc(consts, 1)
            pool.wait_ge(consts, 12)
            pool.affine_select(out=sel[:, :, :], in_=sel[:, :, :], compare_op=ALU.is_ge, fill=0.0,
                               base=0, pattern=[[-3, TILES], [0, P]], channel_multiplier=1).then_inc(consts, 1)
            pool.wait_ge(consts, 13)
            pool.affine_select(out=sel[:, :, :], in_=sel[:, :, :], compare_op=ALU.is_ge, fill=0.0,
                               base=2, pattern=[[3, TILES], [0, P]], channel_multiplier=-1).then_inc(consts, 1)
            pool.wait_ge(consts, 14)

            pool.wait_ge(table_out, 16 * (len(STEPS) + 1))
            pool.wait_ge(xT_ps, len(STEPS))

            def gather(third, before, prev, b, nxt, ahead):
                if follows(b, BUFS):
                    pool.wait_ge(summed[0], b.n - (BUFS - 1))
                pool.wait_ge(index_in[b.four], (b.fours + 1) * 64)
                n = pool.value_load(count_i[0:1, b.n:b.n + 1] if b.known else count_i[0:1, bass.ds(b.n, 1)],
                                    min_val=0, max_val=E)
                for c, tiles in enumerate(CHUNKS):
                    if c and follows(b, BUFS):
                        pool.wait_ge(consts, 14)
                        pool.wait_ge(summed[c], b.n - (BUFS - 1))
                    for g in tiles:
                        def rows():
                            pool.indirect_dma_start(got[b.four][:, g, 0:2 * D], None, table,
                                                    bass.IndirectOffsetOnAxis(ap=src_i[b.four][:, g:g + 1], axis=0),
                                                    bounds_check=N - 1, oob_is_err=True)\
                                .then_inc(gathered[b.four][c], 16)
                        if g <= MAIN:
                            rows()
                        else:
                            with pool.If(n > g * P):
                                rows()
                            with pool.Else():
                                pool.inc_swdge_sem([gathered[b.four][c]], [16], mode="add")

            def general_tile(t):
                def rows(k, tile, source, index):
                    pool.indirect_dma_start(tile, None, source, bass.IndirectOffsetOnAxis(ap=index, axis=0),
                                            bounds_check=source.shape[0] - 1, oob_is_err=True).then_inc(g_got[k], 16)

                loads, tiles = pool.to_reg((t + 1) * 16), pool.to_reg(t + 1)
                pool.wait_ge(consts, 14)
                pool.wait_ge(g_in[1], loads)
                pool.wait_ge(g_in[2], loads)
                rows(0, g_source, table, g_src)
                rows(1, g_target, table, g_dst)
                rows(2, g_old, state, g_dst)
                pool.wait_ge(consts, 14)
                pool.wait_ge(g_new_done, tiles)
                pool.indirect_dma_start(state, bass.IndirectOffsetOnAxis(ap=g_to, axis=0), g_new, None,
                                        bounds_check=state.shape[0] - 1, oob_is_err=True).then_inc(g_put, 16)

            with pool.If(is_general(pool)):
                pool.memset(g_lower, 1.0).then_inc(g_lower_set, 1)
                pool.wait_ge(g_lower_set, 1)
                pool.affine_select(out=g_lower, in_=g_lower, compare_op=ALU.is_gt, fill=0.0,
                                   base=0, pattern=[[-1, LANES]], channel_multiplier=1).then_inc(g_lower_set, 1)
                pool.iota(g_to, pattern=[[0, 1]], base=N, channel_multiplier=1).then_inc(g_lower_set, 1)
                pool.wait_ge(g_fresh, 2)
                pool.dma_start(state.rearrange("(p c) d -> p c d", p=P),
                               state_piece[0][:, 0:1, :].to_broadcast([P, BLOCKS + 1, STATE])).then_inc(g_put, 16)
                pool.wait_ge(g_put, 16)
                with pool.Fori(0, E // LANES) as t:
                    general_tile(t)
            with pool.Else():
                pipeline(pool, gather)
            pool.wait_ge(rstd_ready, 1)
            for k, (a, z) in enumerate(POOLED):
                normalise(pool, a, z, pool_centred, pool_normed, k + 1)

        @block.scalar
        def _(act):
            act.wait_ge(w_ps, 1)
            act.activation(watt2T[:, :], ps_misc[:, 0:P], ACT.Copy).then_inc(w_sb, 1)

            def copy_xT(s):
                n = len(STEPS[s]) * D
                act.wait_ge(xT_ps, s + 1)
                if s >= 2:
                    act.wait_ge(h_ps, s - 1)
                act.activation(xT[s % 2][:, 0:n], ps_hd[s % 2][:, 0:n], ACT.Copy).then_inc(xT_sb, 1)

            def split_h(s, part):
                a, z = STEPS[s][0], STEPS[s][-1] + 1
                if part == 0:
                    act.wait_ge(h_sb, s + 1)
                    h, scale = hx[:, a:z, 0:D], SCALE
                else:
                    act.wait_ge(rest_done[part - 1], s + 1)
                    h, scale = h_rest(s, part - 1), 1.0
                act.activation(h3[:, a:z, part, :], h, ACT.Copy, scale=scale).then_inc(part_done[part], 1)

            for s in range(len(STEPS) + 2 + LAG):
                if s < len(STEPS):
                    copy_xT(s)
                for part in range(3):
                    if 0 <= s - LAG - part < len(STEPS):
                        split_h(s - LAG - part, part)
                if s == FIRST_STEP:
                    act.wait_ge(first_ps, 1)
                    act.activation(first_row[0:1, :], ps_acc[0:1, 0:P + 1], ACT.Copy).then_inc(first_sb, 1)
            act.wait_ge(w_ps, 2)
            act.activation(w12T[:, :], ps_misc[:, 0:D], ACT.Copy).then_inc(w_sb, 1)

            def copy_hot(b, chunks):
                for c in chunks:
                    a, z = cols(c)
                    act.wait_ge(other_ps[c], b.n + 1)
                    ps = ps_other[(b.two + c) % 2][:, 0:(z - a) * P].rearrange("p (g e) -> p g e", e=P)
                    act.activation(hotT[b.four][:, a:z, :], ps, ACT.Copy, bias=1.0, scale=-1.0)\
                        .then_inc(hot_sb[c], 1)

            def tanh(b, c):
                a, z = cols(c)
                act.wait_ge(added[c], b.n + 1)
                act.activation(edge[b.two][:, a:z, :], edge[b.two][:, a:z, :], ACT.Tanh).then_inc(tanh_done[c], 1)

            def weigh(b, chunks):
                for c in chunks:
                    if c == 0:
                        act.wait_ge(arg_done, b.n + 1)
                    if follows(b, 1):
                        act.wait_ge(summed[c], b.n)
                    for g in CHUNKS[c]:
                        last = act.activation(weight[:, g, :], other[b.four][:, g, :], ACT.Exp,
                                              bias=arg[b.two][:, g:g + 1], scale=-MASKED)
                    last.then_inc(weights_done[c], 1)

            def copy_scores(b):
                act.wait_ge(sT_ps, b.n + 1)
                act.activation(score3T[:, :], a_sT, ACT.Copy).then_inc(sT_sb, 1)

            def copy_sum_prod(b):
                act.wait_ge(spT_ps, b.n + 1)
                act.activation(sum_prodT[:, :], m_spT, ACT.Copy).then_inc(spT_sb, 1)

            def deviations(k):
                a, z = DEVIATED[k]
                act.wait_ge(y_done, z)
                act.activation(std[:, a:z], stats[:, a:z, 1], ACT.Sqrt, bias=eps_col[:, 0:1]).then_inc(std_ready, 1)

            def step(third, before, prev, b, nxt, ahead):
                if exists(before):
                    weigh(before, (0,))
                if exists(prev):
                    copy_scores(prev)
                tanh(b, 0)
                if exists(before):
                    weigh(before, (1,))
                tanh(b, 1)
                if exists(before):
                    weigh(before, (2, 3))
                tanh(b, 2)
                if exists(before):
                    weigh(before, (4,))
                tanh(b, 3)
                if exists(nxt):
                    copy_hot(nxt, (0, 1))
                tanh(b, 4)
                if exists(nxt):
                    copy_hot(nxt, (2,))
                if exists(before):
                    copy_sum_prod(before)
                if exists(nxt):
                    copy_hot(nxt, (3, 4))
                if b.known and b.n == LAST - 1:
                    deviations(0)

            def general_tile(t):
                act.wait_ge(g_added, t + 1)
                act.activation(g_edge, g_edge, ACT.Tanh).then_inc(g_tanh_done, 1)
                act.wait_ge(g_args, t + 1)
                act.activation(g_prob, g_arg, ACT.Exp)
                act.activation(g_keep, g_fade, ACT.Exp).then_inc(g_exps, 1)

            with act.If(is_general(act)):
                with act.Fori(0, E // LANES) as t:
                    general_tile(t)
                piece_blocks(act, lambda b, k, i: copy_sum_prod(b))
                for k in range(len(DEVIATED)):
                    deviations(k)
            with act.Else():
                copy_hot(at_block(0, 0), range(NC))
                pipeline(act, step)
                last, prev = at_block(0, LAST), at_block(0, LAST - 1)
                weigh(prev, (0, 1))
                copy_scores(last)
                weigh(prev, (2, 3, 4))
                weigh(last, (0, 1))
                copy_sum_prod(prev)
                weigh(last, (2, 3, 4))
                deviations(1)
                copy_sum_prod(last)
                deviations(2)

        @block.tensor
        def _(pe):
            pe.wait_ge(consts, 6)
            pe.wait_ge(watt_in, 32)
            pe.transpose(ps_misc[:, 0:P], watt2[:, :], ident[:, :]).then_inc(w_ps, 1)

            def transpose_x(s):
                if s % (PIECE // STEP) == 0 and s // (PIECE // STEP) < PIECES:
                    k = s // (PIECE // STEP)
                    pe.wait_ge(x_in[k], 16 if k < PIECES - 1 else 32)
                if s >= 2:
                    pe.wait_ge(xT_sb, s - 1)
                for k in range(0, len(STEPS[s]), 2):
                    b = STEPS[s][k]
                    p = min(b // PIECE, PIECES - 1)
                    last = pe.transpose(ps_hd[s % 2][:, k * D:(k + 2) * D], 
                                        x_piece[p][:, b - p * PIECE:b - p * PIECE + 2, :].rearrange("p b d -> p (b d)"),
                                        ident[:, :])
                last.then_inc(xT_ps, 1)

            def project(s):
                pe.wait_ge(xT_sb, s + 1)
                if s >= 2:
                    pe.wait_ge(h_sb, s - 1)
                for k in range(0, len(STEPS[s]), 2):
                    last = pe.matmul(ps_sc[s % 2][:, k * D:(k + 2) * D], xT[s % 2][:, k * D:(k + 2) * D],
                                     watt2T[:, :], start=True, stop=True)
                last.then_inc(h_ps, 1)

            for s in range(len(STEPS)):
                transpose_x(s)
                if s == 0:
                    pe.wait_ge(w_sb, 1)
                if s >= 1:
                    project(s - 1)
                if s == ROW_STEP:
                    pe.wait_ge(rows_counted, 1)
                    pe.matmul(ps_acc[0:BLOCKS + 1, 0:1], below_row[0:ROWS, 0:BLOCKS + 1], ones[0:ROWS, :],
                              start=True, stop=True).then_inc(row_ps, 1)
                if s == FIRST_STEP:
                    pe.wait_ge(first_ready, 1)
                    pe.transpose(ps_acc[0:1, 0:P], first[:, :], ident[:, :])
                    pe.wait_ge(falls_ready, 1)
                    pe.matmul(ps_acc[0:1, P:P + 1], falls[0:ROWS, :], ones[0:ROWS, :],
                              start=True, stop=True).then_inc(first_ps, 1)
            project(len(STEPS) - 1)
            pe.wait_ge(w12_in, 32)
            pe.transpose(ps_misc[:, 0:D], w12[:, :, :].rearrange("o a i -> o (a i)"),
                         ident[0:D, 0:D]).then_inc(w_ps, 1)

            def transpose_other(b, chunks):
                if 0 in chunks:
                    pe.wait_ge(other_built, b.n + 1)
                for c in chunks:
                    if c >= 2:
                        pe.wait_ge(hot_sb[c - 2], b.n + 1)
                    elif follows(b, 1):
                        pe.wait_ge(hot_sb[c - 2 + NC], b.n)
                    for k, g in enumerate(CHUNKS[c]):
                        last = pe.transpose(ps_other[(b.two + c) % 2][:, k * P:(k + 1) * P],
                                            other[b.four][:, g, :], ident16[:, :])
                    last.then_inc(other_ps[c], 1)

            def expand(b, c):
                pe.wait_ge(hot_sb[c], b.n + 1)
                if c >= 2:
                    pe.wait_ge(scored[c - 2], b.n + 1)
                elif follows(b, 1):
                    pe.wait_ge(scored[c - 2 + NC], b.n)
                for k, g in enumerate(CHUNKS[c]):
                    for part in range(3):
                        rhs = h3[:, b.n, part, :] if b.known else \
                            h3[:, bass.ds(b.n, 1), part, :].rearrange("p a d -> p (a d)")
                        last = pe.matmul(ps_hd[(b.two + c) % 2][:, k * D:(k + 1) * D], hotT[b.four][:, g, :], rhs,
                                         start=(part == 0), stop=(part == 2))
                last.then_inc(hd_ready[c], 1)

            def transpose_scores(b):
                pe.wait_ge(consts, 14)
                pe.wait_ge(split_done, b.n + 1)
                pe.transpose(a_sT, score3[:, :, :].rearrange("p g s -> p (g s)"), ident16[:, :]).then_inc(sT_ps, 1)

            def spread_scores(b, chunks):
                pe.wait_ge(sT_sb, b.n + 1)
                for c in chunks:
                    if c >= 2:
                        pe.wait_ge(sc_used[c - 2], b.n + 1)
                    elif follows(b, 1):
                        pe.wait_ge(sc_used[c - 2 + NC], b.n)
                    for k, g in enumerate(CHUNKS[c]):
                        spread = ps_sc[(b.two + c) % 2][:, k * P:(k + 1) * P]
                        pe.matmul(spread, other[b.four][:, g, :], mask16[:, :], start=True, stop=False)
                        last = pe.matmul(spread, sel[:, g, :], score3T[:, :], start=False, stop=True)
                    last.then_inc(sc_ready[c], 1)

            def spread_max(b):
                pe.wait_ge(max_split, b.n + 1)
                for g in range(TILES):
                    last = pe.matmul(m_max[:, 3 * g:3 * g + 3], hotT[b.four][:, g, :], max3[:, :],
                                     start=True, stop=True)
                last.then_inc(max_ps, 1)

            def sum_edges(b, chunks):
                for c in chunks:
                    if c == 0 and follows(b, 1):
                        pe.wait_ge(own["z1"], b.n)
                    pe.wait_ge(weights_done[c], b.n + 1)
                    for g in CHUNKS[c]:
                        last = pe.matmul(a_sum, weight[:, g, :], got[b.four][:, g, D:2 * D + 1],
                                         start=(g == 0), stop=(g == TILES - 1))
                    last.then_inc(summed[c], 1)

            def transpose_sum_prod(b):
                pe.wait_ge(sp_done, b.n + 1)
                pe.transpose(m_spT, sum_prod[:, :], ident[:, :]).then_inc(spT_ps, 1)

            def dense(b):
                pe.wait_ge(spT_sb, b.n + 1)
                pe.matmul(a_out, sum_prodT[:, :], w12T[:, :], start=True, stop=True).then_inc(out_ps, 1)

            pe.wait_ge(h3_ready, 1)
            pe.wait_ge(ones_set, BUFS)
            pe.wait_ge(w_sb, 2)

            def step(third, before, prev, b, nxt, ahead):
                if exists(third):
                    dense(third)
                expand(b, 0)
                if exists(prev):
                    transpose_scores(prev)
                expand(b, 1)
                if exists(prev):
                    spread_scores(prev, (0, 1))
                if exists(before):
                    sum_edges(before, (0,))
                if exists(prev):
                    spread_scores(prev, (2, 3))
                if exists(before):
                    sum_edges(before, (1,))
                if exists(prev):
                    spread_scores(prev, (4,))
                expand(b, 2)
                if exists(before):
                    sum_edges(before, (2, 3))
                if exists(prev):
                    spread_max(prev)
                if exists(before):
                    sum_edges(before, (4,))
                if exists(nxt):
                    transpose_other(nxt, (0, 1))
                expand(b, 3)
                if exists(nxt):
                    transpose_other(nxt, (2,))
                expand(b, 4)
                if exists(before):
                    transpose_sum_prod(before)
                if exists(nxt):
                    transpose_other(nxt, (3, 4))

            def general_tile(t):
                pe.wait_ge(g_wide, t + 1)
                pe.transpose(ps_hd[0][0:LANES, 0:LANES], g_dst_wide, ident[0:LANES, 0:LANES])
                pe.transpose(ps_hd[1][0:LANES, 0:LANES], g_score_wide, ident[0:LANES, 0:LANES])\
                    .then_inc(g_wide_ps, 1)
                pe.wait_ge(g_sent_done, t + 1)
                pe.matmul(ps_sc[0][0:LANES, 0:D + 1], g_same, g_sent, start=True, stop=True).then_inc(g_sums_ps, 1)

            def general_block(b, k, i):
                pe.matmul(a_sum, ident[:, :], state_piece[k][:, bass.ds(i, 1), 0:D + 1].rearrange("p a d -> p (a d)"),
                          start=True, stop=True).then_inc(summed[NC - 1], 1)
                transpose_sum_prod(b)
                dense(b)
                pe.wait_ge(own["z1"], b.n + 1)

            with pe.If(is_general(pe)):
                with pe.Fori(0, E // LANES) as t:
                    general_tile(t)
                pe.wait_ge(g_back, 16 * PIECES)
                piece_blocks(pe, general_block)
            with pe.Else():
                transpose_other(at_block(0, 0), range(NC))
                pipeline(pe, step)
                last, prev = at_block(0, LAST), at_block(0, LAST - 1)
                dense(at_block(0, LAST - 2))
                transpose_scores(last)
                spread_scores(last, range(NC))
                sum_edges(prev, (0,))
                spread_max(last)
                sum_edges(prev, range(1, NC))
                transpose_sum_prod(prev)
                dense(prev)
                sum_edges(last, range(NC))
                transpose_sum_prod(last)
                dense(last)

        @block.vector
        def _(dve):
            done = [0]

            def link(ins):
                done[0] += 1
                ins.then_inc(dve_c, 1)
                dve.wait_ge(dve_c, done[0])

            dve.memset(ones[:, :], 1.0)
            dve.memset(eps_col[:, :], EPS_NORM)
            dve.memset(first[:, :], 0.0)
            dve.memset(base[:, :], 0.0)
            dve.wait_ge(consts, 4)
            dve.tensor_copy(bound[:, :], bound_i[:, :])
            link(dve.tensor_copy(bound_row[:, :], bound_row_i[:, :]))
            dve.wait_ge(rows_in, 16)
            link(dve.tensor_copy(row_last[0:ROWS, :], rows_i[0:ROWS, SEARCH_ROW - 1:SEARCH_ROW]))
            dve.tensor_scalar(below_row[0:ROWS, :], bound_row[0:ROWS, :], row_last[0:ROWS, 0:1], None,
                              ALU.is_gt).then_inc(rows_counted, 1)
            dve.memset(falls[:, :], 0.0)
            link(dve.tensor_tensor(falling[0:ROWS, :], rows_i[0:ROWS, 0:SEARCH_ROW - 1], rows_i[0:ROWS, 1:SEARCH_ROW],
                                   ALU.is_gt))
            link(dve.tensor_reduce(falls[0:ROWS, :], falling[0:ROWS, :], AX.X, ALU.add))
            dve.wait_ge(next_in, 16)
            link(dve.tensor_tensor(row_falls[0:ROWS - 1, :], row_last[0:ROWS - 1, :], next_first[0:ROWS - 1, :],
                                   ALU.is_gt))
            dve.tensor_tensor(falls[0:ROWS - 1, :], falls[0:ROWS - 1, :], row_falls[0:ROWS - 1, :], ALU.add)\
                .then_inc(falls_ready, 1)
            dve.wait_ge(consts, 7)
            dve.tensor_copy(ident16[:, :], ident[:, :])
            dve.tensor_scalar(mask16[:, :], ident[:, :], -MASKED, None, ALU.mult)
            link(dve.tensor_copy(iota_h[:, :], iota_i[:, :]))

            BOUNDS = BLOCKS + 1

            def pick_rows():
                dve.wait_ge(row_ps, 1)
                link(dve.tensor_scalar(row_f[0:BOUNDS, :], ps_acc[0:BOUNDS, 0:1], float(ROWS - 1), None, ALU.min))
                dve.tensor_copy(row_idx[0:BOUNDS, :], row_f[0:BOUNDS, :]).then_inc(row_ready, 1)

            def find_first():
                dve.wait_ge(rows_got, 16)
                link(dve.tensor_scalar(below[0:BOUNDS, :], rows_i[0:BOUNDS, :], bound[0:BOUNDS, 0:1], None,
                                       ALU.is_lt))
                link(dve.tensor_reduce(below_n[0:BOUNDS, :], below[0:BOUNDS, :], AX.X, ALU.add))
                dve.scalar_tensor_tensor(out=first[0:BOUNDS, :], in0=row_f[0:BOUNDS, :], scalar=float(SEARCH_ROW),
                                         in1=below_n[0:BOUNDS, :], op0=ALU.mult, op1=ALU.add)\
                    .then_inc(first_ready, 1)

            def set_windows():
                dve.wait_ge(first_sb, 1)
                link(dve.tensor_scalar(start_row[:, :], first_row[:, 0:P], float(E - WINDOW), None, ALU.min))
                link(dve.tensor_tensor(count_row[:, 0:BLOCKS], first_row[:, 1:BOUNDS], start_row[:, 0:BLOCKS],
                                       ALU.subtract))
                link(dve.tensor_scalar(over_row[:, 0:BLOCKS], count_row[:, 0:BLOCKS], float(WINDOW), None, ALU.is_gt))
                link(dve.tensor_reduce(over[:, :], over_row[:, 0:BLOCKS], AX.X, ALU.add))
                link(dve.tensor_tensor(general[:, :], over[:, :], first_row[:, P:P + 1], ALU.add))
                dve.tensor_copy(general_i[:, :], general[:, :])
                link(dve.tensor_copy(start_i[:, 0:BLOCKS], start_row[:, 0:BLOCKS]))
                dve.tensor_copy(count_i[:, 0:BLOCKS], count_row[:, 0:BLOCKS]).then_inc(windows_ready, 1)

            def step_h(s):
                a, z = STEPS[s][0], STEPS[s][-1] + 1
                dve.wait_ge(h_ps, s + 1)
                dve.tensor_tensor(hx[:, a:z, 0:D], ps_sc[s % 2][:, 0:(z - a) * D].rearrange("p (b d) -> p b d", d=D),
                                  batt_bc[:, :].rearrange("p (a d) -> p a d", a=1).to_broadcast([P, z - a, D]),
                                  ALU.add).then_inc(h_sb, 1)

            def rest_of_h(s, part):
                a, z = STEPS[s][0], STEPS[s][-1] + 1
                dve.wait_ge(part_done[part], s + 1)
                if s >= 2:
                    dve.wait_ge(part_done[part + 1], s - 1)
                if part == 0:
                    if s >= 2:
                        dve.wait_ge(rest_done[1], s - 1)
                    dve.scalar_tensor_tensor(out=h_rest(s, 0), in0=hx[:, a:z, 0:D], scalar=SCALE,
                                             in1=h3[:, a:z, 0, :], op0=ALU.mult, op1=ALU.subtract)\
                        .then_inc(rest_done[0], 1)
                else:
                    dve.wait_ge(rest_done[0], s + 1)
                    dve.tensor_tensor(h_rest(s, 1), h_rest(s, 0), h3[:, a:z, 1, :], ALU.subtract)\
                        .then_inc(rest_done[1], 1)

            pick_rows()
            dve.wait_ge(batt_in, 16)
            for s in range(len(STEPS) + 1 + LAG):
                if s < len(STEPS):
                    step_h(s)
                if s == FIRST_STEP - 1:
                    find_first()
                if s == WINDOW_STEP:
                    set_windows()
                for part in range(2):
                    if 0 <= s - LAG - part < len(STEPS):
                        rest_of_h(s - LAG - part, part)
            dve.wait_ge(part_done[2], len(STEPS))
            dve.wait_ge(bias_in, 32)
            dve.tensor_tensor(b12[:, :], b1_bc[:, :], b2_bc[:, :], ALU.add).then_inc(h3_ready, 1)
            dve.wait_ge(h3_ready, 1)
            dve.wait_ge(x_set, PIECES)
            dve.wait_ge(xT_ps, len(STEPS))
            for k in range(BUFS):
                dve.memset(got[k][:, :, 2 * D:2 * D + 1], 1.0).then_inc(ones_set, 1)

            def chain(name, ins, b):
                ins.then_inc(own[name], 1)
                dve.wait_ge(own[name], b.n + 1)

            def build_other(b):
                dve.wait_ge(index_in[b.four], (b.fours + 1) * 64)
                if follows(b, BUFS):
                    dve.wait_ge(weights_done[NC - 1], b.n - (BUFS - 1))
                chain("rel", dve.tensor_scalar(
                    dst_rel[:, :, :], dst_i[b.four][:, :].rearrange("p (g a) -> p g a", a=1).to_broadcast([P, TILES, 2]),
                    base[:, 0:1], None, ALU.subtract), b)
                chain("base", dve.tensor_scalar(base[:, :], base[:, :], float(P), None, ALU.add), b)
                dve.tensor_tensor(
                    other[b.four][:, :, :].rearrange("p g (n a) -> p g n a", a=2),
                    iota_h[:, :].rearrange("p (z n a) -> p z n a", z=1, a=2).to_broadcast([P, TILES, P // 2, 2]),
                    dst_rel[:, :, :].rearrange("p g (z a) -> p g z a", z=1).to_broadcast([P, TILES, P // 2, 2]),
                    ALU.not_equal).then_inc(other_built, 1)

            def add(b, c):
                a, z = cols(c)
                if c == 0:
                    dve.wait_ge(edge_in[b.two], (b.twos + 1) * 32)
                dve.wait_ge(gathered[b.four][c], (b.fours + 1) * (16 * (z - a)))
                dve.tensor_tensor(edge[b.two][:, a:z, :], edge[b.two][:, a:z, :], got[b.four][:, a:z, 0:D],
                                  ALU.add).then_inc(added[c], 1)

            def dot(b, c):
                a, z = cols(c)
                dve.wait_ge(consts, 14)
                dve.wait_ge(tanh_done[c], b.n + 1)
                dve.wait_ge(hd_ready[c], b.n + 1)
                for k, g in enumerate(CHUNKS[c]):
                    last = dve.tensor_tensor_reduce(
                        out=edge[b.two][:, g, :], in0=edge[b.two][:, g, :],
                        in1=ps_hd[(b.two + c) % 2][:, k * D:(k + 1) * D], scale=1.0, scalar=0.0,
                        op0=ALU.mult, op1=ALU.add, accum_out=raw[b.two][:, g:g + 1])
                last.then_inc(scored[c], 1)

            def finish_scores(b):
                dve.wait_ge(scored[NC - 1], b.n + 1)
                chain("score", dve.scalar_tensor_tensor(out=score[:, :], in0=raw[b.two][:, :], scalar=SLOPE,
                                                        in1=raw[b.two][:, :], op0=ALU.mult, op1=ALU.max), b)
                chain("s0", dve.tensor_copy(score3[:, :, 0], score[:, :]), b)
                chain("r1", dve.tensor_tensor(rest1[:, :], score[:, :], score3[:, :, 0], ALU.subtract), b)
                chain("s1", dve.tensor_copy(score3[:, :, 1], rest1[:, :]), b)
                chain("r2", dve.tensor_tensor(rest2[:, :], rest1[:, :], score3[:, :, 1], ALU.subtract), b)
                dve.tensor_copy(score3[:, :, 2], rest2[:, :]).then_inc(split_done, 1)

            def take_max(b, chunks):
                for c in chunks:
                    a, z = cols(c)
                    dve.wait_ge(sc_ready[c], b.n + 1)
                    dve.tensor_reduce(chunk_max[:, c:c + 1], ps_sc[(b.two + c) % 2][:, 0:(z - a) * P], AX.X, ALU.max)\
                        .then_inc(sc_used[c], 1)

            def split_max(b):
                dve.wait_ge(sc_used[NC - 1], b.n + 1)
                chain("nmax", dve.tensor_reduce(node_max[:, :], chunk_max[:, :], AX.X, ALU.max), b)
                chain("m0", dve.tensor_copy(max3[:, 0:1], node_max[:, :]), b)
                chain("q1", dve.tensor_tensor(mrest1[:, :], node_max[:, :], max3[:, 0:1], ALU.subtract), b)
                chain("m1", dve.tensor_copy(max3[:, 1:2], mrest1[:, :]), b)
                chain("q2", dve.tensor_tensor(mrest2[:, :], mrest1[:, :], max3[:, 1:2], ALU.subtract), b)
                dve.tensor_copy(max3[:, 2:3], mrest2[:, :]).then_inc(max_split, 1)

            def exponents(b):
                dve.wait_ge(max_ps, b.n + 1)
                if follows(b, 2):
                    dve.wait_ge(weights_done[NC - 1], b.n - 1)
                chain("emax", dve.tensor_reduce(edge_max[:, :], m_max.rearrange("p (g s) -> p g s", s=3),
                                                AX.X, ALU.add), b)
                dve.tensor_tensor(arg[b.two][:, :], score[:, :], edge_max[:, :], ALU.subtract).then_inc(arg_done, 1)

            def neighbours(b):
                dve.wait_ge(summed[NC - 1], b.n + 1)
                chain("den", dve.tensor_scalar(den[:, :], a_sum[:, D:D + 1], EPS_ALPHA, None, ALU.add), b)
                chain("rden", dve.reciprocal(rden[:, :], den[:, :]), b)
                dve.tensor_scalar(h_neigh[:, :], a_sum[:, 0:D], rden[:, 0:1], None, ALU.mult)\
                    .then_inc(h_neigh_done, 1)
                dve.wait_ge(h_neigh_done, b.n + 1)
                xb = node_rows(hx, b, D, 2 * D)
                dve.tensor_tensor(sum_prod[:, 0:D], h_neigh[:, :], xb, ALU.add)
                dve.tensor_tensor(sum_prod[:, D:2 * D], h_neigh[:, :], xb, ALU.mult).then_inc(sp_done, 1)

            def residual(b, part):
                if part == 0:
                    dve.wait_ge(out_ps, b.n + 1)
                    dve.tensor_tensor(z1[:, :], a_out, b12[:, :], ALU.add).then_inc(own["z1"], 1)
                    return
                dve.wait_ge(own["z1"], b.n + 1)
                chain("z2", dve.scalar_tensor_tensor(out=z2[:, :], in0=z1[:, :], scalar=SLOPE, in1=z1[:, :],
                                                     op0=ALU.mult, op1=ALU.max), b)
                chain("y", dve.tensor_tensor(y_new[:, :], node_rows(hx, b, D, 2 * D), z2[:, :], ALU.add), b)
                dve.bn_stats(bn6[:, :], y_new[:, :]).then_inc(own["bn"], 1)
                dve.tensor_copy(node_rows(hx, b, 0, D), y_new[:, :])
                dve.wait_ge(consts, 14)
                dve.wait_ge(own["bn"], b.n + 1)
                chain("aggr", dve.bn_aggr(mean_var[:, :], bn6[:, :]), b)
                dve.tensor_copy(node_rows(stats, b, 0, 2), mean_var[:, :]).then_inc(y_done, 1)

            def invert(k):
                a, z = DEVIATED[k]
                dve.wait_ge(std_ready, k + 1)
                dve.reciprocal(rstd[:, a:z], std[:, a:z]).then_inc(rstd_ready, 1)

            def normalise_part(k):
                invert(k + 1)
                dve.wait_ge(rstd_ready, k + 2)
                normalise(dve, *NORMED[k], centred, normed, k + 1)

            def step(third, before, prev, b, nxt, ahead):
                if exists(third):
                    residual(third, 0)
                if exists(prev):
                    finish_scores(prev)
                if exists(third):
                    residual(third, 1)
                add(b, 0)
                if exists(prev):
                    take_max(prev, (0,))
                add(b, 1)
                if exists(prev):
                    take_max(prev, (1,))
                dot(b, 0)
                if exists(prev):
                    take_max(prev, (2,))
                add(b, 2)
                if exists(prev):
                    take_max(prev, (3,))
                dot(b, 1)
                if exists(prev):
                    take_max(prev, (4,))
                    split_max(prev)
                if exists(nxt):
                    build_other(nxt)
                dot(b, 2)
                add(b, 3)
                if exists(prev):
                    exponents(prev)
                add(b, 4)
                if exists(before):
                    neighbours(before)
                dot(b, 3)
                dot(b, 4)

            LINKS = 19

            def general_tile(t):
                links = [0]

                def own_next(ins):
                    links[0] += 1
                    ins.then_inc(g_own, 1)
                    dve.wait_ge(g_own, t * LINKS + links[0])

                dve.wait_ge(g_in[2], (t + 1) * 16)
                own_next(dve.tensor_copy(g_dst_f, g_dst))
                own_next(dve.tensor_copy(g_dst_wide, g_dst_f.to_broadcast([LANES, LANES])))
                dve.wait_ge(g_in[0], (t + 1) * 16)
                for k in range(3):
                    dve.wait_ge(g_got[k], (t + 1) * 16)
                dve.tensor_tensor(g_edge, g_edge, g_source[:, 0:D], ALU.add).then_inc(g_added, 1)
                dve.wait_ge(g_tanh_done, t + 1)
                own_next(dve.tensor_tensor(g_edge, g_edge, g_target[:, 0:D], ALU.mult))
                own_next(dve.tensor_reduce(g_raw, g_edge, AX.X, ALU.add))
                own_next(dve.tensor_scalar(g_scaled, g_raw, SCALE, None, ALU.mult))
                own_next(dve.scalar_tensor_tensor(out=g_score, in0=g_scaled, scalar=SLOPE, in1=g_scaled,
                                                  op0=ALU.mult, op1=ALU.max))
                dve.tensor_copy(g_score_wide, g_score.to_broadcast([LANES, LANES])).then_inc(g_wide, 1)
                dve.wait_ge(g_wide_ps, t + 1)
                own_next(dve.tensor_scalar(g_same, ps_hd[0][0:LANES, 0:LANES], g_dst_f, None, ALU.is_equal))
                own_next(dve.tensor_scalar(g_far, ps_hd[0][0:LANES, 0:LANES], g_dst_f, -MASKED,
                                           ALU.not_equal, ALU.mult))
                own_next(dve.tensor_tensor(g_far, g_far, ps_hd[1][0:LANES, 0:LANES], ALU.add))
                own_next(dve.tensor_reduce(g_most, g_far, AX.X, ALU.max))
                own_next(dve.tensor_tensor(g_new[:, D + 1:D + 2], g_most, g_old[:, D + 1:D + 2], ALU.max))
                own_next(dve.tensor_tensor(g_arg, g_score, g_new[:, D + 1:D + 2], ALU.subtract))
                dve.tensor_tensor(g_fade, g_old[:, D + 1:D + 2], g_new[:, D + 1:D + 2], ALU.subtract)\
                    .then_inc(g_args, 1)
                own_next(dve.tensor_tensor(g_before, g_same, g_lower, ALU.mult))
                own_next(dve.tensor_reduce(g_earlier, g_before, AX.X, ALU.max))
                own_next(dve.tensor_tensor(g_rise, g_slot, g_dst_f, ALU.subtract))
                own_next(dve.tensor_tensor(g_move, g_rise, g_earlier, ALU.mult))
                own_next(dve.tensor_tensor(g_scaled, g_dst_f, g_move, ALU.add))
                own_next(dve.tensor_copy(g_to, g_scaled))
                dve.wait_ge(g_exps, t + 1)
                dve.tensor_copy(g_sent[:, D:D + 1], g_prob)
                dve.tensor_scalar(g_sent[:, 0:D], g_source[:, D:2 * D], g_prob, None, ALU.mult)\
                    .then_inc(g_sent_done, 1)
                own_next(dve.tensor_scalar(g_new[:, 0:D + 1], g_old[:, 0:D + 1], g_keep, None, ALU.mult))
                dve.wait_ge(g_sums_ps, t + 1)
                dve.tensor_tensor(g_new[:, 0:D + 1], g_new[:, 0:D + 1], ps_sc[0][0:LANES, 0:D + 1], ALU.add)\
                    .then_inc(g_new_done, 1)
                assert links[0] == LINKS, links

            def general_block(b, k, i):
                neighbours(b)
                residual(b, 0)
                residual(b, 1)

            with dve.If(is_general(dve)):
                dve.memset(state_piece[0][:, 0, 0:D + 1], 0.0).then_inc(g_fresh, 1)
                dve.memset(state_piece[0][:, 0, D + 1:D + 2], LOWEST).then_inc(g_fresh, 1)
                dve.wait_ge(g_lower_set, 3)
                link(dve.tensor_copy(g_slot, g_to))
                with dve.Fori(0, E // LANES) as t:
                    general_tile(t)
                piece_blocks(dve, general_block)
                invert(0)
                for k in range(len(NORMED)):
                    normalise_part(k)
            with dve.Else():
                build_other(at_block(0, 0))
                pipeline(dve, step)
                last, prev = at_block(0, LAST), at_block(0, LAST - 1)
                invert(0)
                residual(at_block(0, LAST - 2), 0)
                finish_scores(last)
                residual(at_block(0, LAST - 2), 1)
                take_max(last, range(NC))
                split_max(last)
                exponents(last)
                neighbours(prev)
                residual(prev, 0)
                residual(prev, 1)
                normalise_part(0)
                neighbours(last)
                residual(last, 0)
                residual(last, 1)
                normalise_part(1)


_INS = ['x', 'src', 'dst', 'edge_attr_64', 'L0_gnn_W1_w', 'L0_gnn_W1_b', 'L0_gnn_W2_w', 'L0_gnn_W2_b',
        'L0_gnn_Watt_w', 'L0_gnn_Watt_b']


def kernel(**inputs):
    import numpy as _np
    import concourse.bacc as _bacc
    from concourse.bass_utils import run_bass_kernel_spmd as _run

    nc = _bacc.Bacc("TRN2", target_bir_lowering=False, num_devices=1)
    arrays, args = {}, []
    for name in _INS:
        a = _np.ascontiguousarray(inputs[name])
        arrays[f"in_{name}"] = a
        args.append(nc.dram_tensor(f"in_{name}", a.shape, mybir.dt.from_np(a.dtype), kind="ExternalInput").ap())
    args.append(nc.dram_tensor("out_0", arrays["in_x"].shape, F32, kind="ExternalOutput").ap())
    gnn_layer(nc, *args)
    r = _run(nc, [arrays], core_ids=[0])
    return r.results[0]["out_0"]
```
